# Optimizing a Trainium2 kernel written in Bass

```python
import numpy as np
import jax
import jax.numpy as jnp

def _softmax(x, axis=-1):
    return jax.nn.softmax(x, axis=axis)

def _gelu(x):
    return jax.nn.gelu(x, approximate=True)

def _silu(x):
    return jax.nn.silu(x)

def _sigmoid(x):
    return jax.nn.sigmoid(x)

def _layernorm(x, axis=-1, eps=1e-05):
    m = jnp.mean(x, axis=axis, keepdims=True)
    v = jnp.var(x, axis=axis, keepdims=True)
    return (x - m) / jnp.sqrt(v + eps)

def _scatter_add(tgt, idx, src, axis=0):
    return tgt.at[idx].add(src)

def _segment_sum(src, seg, n):
    return jax.ops.segment_sum(src, seg, n)
kernel_name = 'mk_xattn_ffn_d1_seqx_r4_1e96a1'

def setup_inputs(seed: int=0):
    np.random.seed(seed)
    _w = jnp.asarray

    def _rec_inputs():
        import jax
        import jax.numpy as jnp
        _rk = jax.random.key(seed)
        x = 7.22e-05 + 1 * jax.random.normal(jax.random.fold_in(_rk, 1), (4, 512, 256), jnp.float32)
        _lenS = 512 - jax.random.randint(jax.random.fold_in(_rk, 7), (4,), 0, max(1, 512 // 4) + 1, jnp.int32)
        _lenS2 = 512 - jax.random.randint(jax.random.fold_in(_rk, 8), (4,), 0, max(1, 512 // 4) + 1, jnp.int32)
        _ctx_1024P = jax.random.normal(jax.random.fold_in(_rk, 11), (4, 16, 256), jnp.float32)
        _ctx_1024c = jax.random.dirichlet(jax.random.fold_in(_rk, 511), 0.3 * jnp.ones((16,), jnp.float32), (4, 512))
        _ctx_1024t = jnp.einsum('bsk,bkd->bsd', _ctx_1024c, _ctx_1024P)
        _ctx_1024t = _ctx_1024t * jax.lax.rsqrt(jnp.mean(jnp.square(_ctx_1024t)) + 1e-12) * 0.953939
        ctx_1024 = 4.13588e-05 + 0.999923 * (_ctx_1024t + 0.3 * jax.random.normal(jax.random.fold_in(_rk, 611), (4, 512, 256), jnp.float32))
        return (x, ctx_1024)
    x, ctx_1024 = _rec_inputs()

    def _L0_xattn_setup():
        import jax, jax.numpy as jnp
        import numpy as np
        EMBED_DIM = 256
        HEAD_DIM = 256
        GAMMA = 0.96875
        THETA = 10000.0
        SCALE_BASE = 512.0

        def _dup_interleave(x):
            return jnp.repeat(x, 2, axis=-1)

        def _rotate_half(x):
            x_even = x[..., ::2]
            x_odd = x[..., 1::2]
            return jnp.stack((-x_odd, x_even), axis=-1).reshape(x.shape)

        def _xpos(x, offset=0, inverse_scale=False):
            l = x.shape[-2]
            half = HEAD_DIM // 2
            scale_vec = (jnp.arange(0, HEAD_DIM, 2, dtype=jnp.float32) + 0.4 * HEAD_DIM) / (1.4 * HEAD_DIM)
            pos = jnp.arange(offset, offset + l, dtype=jnp.float32)
            scale = scale_vec[None, :] ** (pos / SCALE_BASE)[:, None]
            freqs = 1.0 / THETA ** (jnp.arange(half, dtype=jnp.float32) / half)
            sin_in = pos[:, None] * freqs[None, :]
            sin, cos = (jnp.sin(sin_in), jnp.cos(sin_in))
            if inverse_scale:
                scale = 1.0 / scale
            return x * _dup_interleave(cos * scale) + _rotate_half(x) * _dup_interleave(sin * scale)

        def _decay_mask(l, gamma):
            idx = jnp.arange(l, dtype=jnp.float32)
            diff = idx[:, None] - idx[None, :]
            return jnp.where(diff >= 0, gamma ** diff, 0.0)
        key = jax.random.key(seed)
        k1, k2, k3, k4, k5, k6 = jax.random.split(key, 6)
        B, L = (4, 512)
        s = 1.0 / np.sqrt(EMBED_DIM)
        return {'q': jax.random.normal(k1, (B, L, EMBED_DIM), dtype=jnp.float32), 'k': jax.random.normal(k2, (B, L, EMBED_DIM), dtype=jnp.float32), 'v': jax.random.normal(k3, (B, L, EMBED_DIM), dtype=jnp.float32), 'Wq': jax.random.normal(k4, (EMBED_DIM, HEAD_DIM), dtype=jnp.float32) * s, 'Wk': jax.random.normal(k5, (EMBED_DIM, HEAD_DIM), dtype=jnp.float32) * s, 'Wv': jax.random.normal(k6, (EMBED_DIM, HEAD_DIM), dtype=jnp.float32) * s}
    _L0_xattn_all = _L0_xattn_setup()
    _L0_xattn_in = {k: v for k, v in _L0_xattn_all.items() if k in ('Wq', 'Wk', 'Wv')}
    del _L0_xattn_all

    def _L0_ffn_setup():
        import jax, jax.numpy as jnp
        import numpy as np
        B, S, D = (4, 128, 256)
        E, K, H = (64, 8, 64)
        ES, HS = (2, 512)
        key = jax.random.key(seed)
        ks = jax.random.split(key, 8)
        scale = 0.02
        rn = lambda k, shape, s: jax.random.normal(k, shape, jnp.float32) * s
        return {'x': rn(ks[0], (B, S, D), 1.0), 'router_w': rn(ks[1], (D, E), scale), 'router_b': jnp.zeros((E,), jnp.float32), 'w1': rn(ks[2], (E, D, H), scale), 'b1': jnp.zeros((E, H), jnp.float32), 'w2': rn(ks[3], (E, H, D), scale), 'b2': jnp.zeros((E, D), jnp.float32), 'sw1': rn(ks[4], (ES, D, HS), scale), 'sb1': jnp.zeros((ES, HS), jnp.float32), 'sw2': rn(ks[5], (ES, HS, D), scale), 'sb2': jnp.zeros((ES, D), jnp.float32)}
    _L0_ffn_all = _L0_ffn_setup()
    _L0_ffn_in = {k: v for k, v in _L0_ffn_all.items() if k in ('router_w', 'router_b', 'w1', 'b1', 'w2', 'b2', 'sw1', 'sb1', 'sw2', 'sb2')}
    del _L0_ffn_all
    return {'x': x, 'ctx_1024': ctx_1024, 'L0_xattn_Wq': _L0_xattn_in['Wq'], 'L0_xattn_Wk': _L0_xattn_in['Wk'], 'L0_xattn_Wv': _L0_xattn_in['Wv'], 'L0_ffn_router_w': _L0_ffn_in['router_w'], 'L0_ffn_router_b': _L0_ffn_in['router_b'], 'L0_ffn_w1': _L0_ffn_in['w1'], 'L0_ffn_b1': _L0_ffn_in['b1'], 'L0_ffn_w2': _L0_ffn_in['w2'], 'L0_ffn_b2': _L0_ffn_in['b2'], 'L0_ffn_sw1': _L0_ffn_in['sw1'], 'L0_ffn_sb1': _L0_ffn_in['sb1'], 'L0_ffn_sw2': _L0_ffn_in['sw2'], 'L0_ffn_sb2': _L0_ffn_in['sb2']}

def reference(x, ctx_1024, L0_xattn_Wq, L0_xattn_Wk, L0_xattn_Wv, L0_ffn_router_w, L0_ffn_router_b, L0_ffn_w1, L0_ffn_b1, L0_ffn_w2, L0_ffn_b2, L0_ffn_sw1, L0_ffn_sb1, L0_ffn_sw2, L0_ffn_sb2):
    import jax
    import jax.numpy as jnp

    def _L0_xattn_ref(q, k, v, Wq, Wk, Wv):
        import jax, jax.numpy as jnp
        import numpy as np
        EMBED_DIM = 256
        HEAD_DIM = 256
        GAMMA = 0.96875
        THETA = 10000.0
        SCALE_BASE = 512.0

        def _dup_interleave(x):
            return jnp.repeat(x, 2, axis=-1)

        def _rotate_half(x):
            x_even = x[..., ::2]
            x_odd = x[..., 1::2]
            return jnp.stack((-x_odd, x_even), axis=-1).reshape(x.shape)

        def _xpos(x, offset=0, inverse_scale=False):
            l = x.shape[-2]
            half = HEAD_DIM // 2
            scale_vec = (jnp.arange(0, HEAD_DIM, 2, dtype=jnp.float32) + 0.4 * HEAD_DIM) / (1.4 * HEAD_DIM)
            pos = jnp.arange(offset, offset + l, dtype=jnp.float32)
            scale = scale_vec[None, :] ** (pos / SCALE_BASE)[:, None]
            freqs = 1.0 / THETA ** (jnp.arange(half, dtype=jnp.float32) / half)
            sin_in = pos[:, None] * freqs[None, :]
            sin, cos = (jnp.sin(sin_in), jnp.cos(sin_in))
            if inverse_scale:
                scale = 1.0 / scale
            return x * _dup_interleave(cos * scale) + _rotate_half(x) * _dup_interleave(sin * scale)

        def _decay_mask(l, gamma):
            idx = jnp.arange(l, dtype=jnp.float32)
            diff = idx[:, None] - idx[None, :]
            return jnp.where(diff >= 0, gamma ** diff, 0.0)
        qh = _xpos(q @ Wq, offset=0, inverse_scale=False)
        kh = _xpos(k @ Wk, offset=0, inverse_scale=True)
        vh = v @ Wv
        L = qh.shape[-2]
        mask = _decay_mask(L, GAMMA)
        scores = jnp.einsum('bld,bmd->blm', qh, kh) * mask[None, :, :]
        return scores @ vh

    def _L0_ffn_ref(x, router_w, router_b, w1, b1, w2, b2, sw1, sb1, sw2, sb2):
        import jax, jax.numpy as jnp
        import numpy as np
        B, S, D = (4, 128, 256)
        E, K, H = (64, 8, 64)
        ES, HS = (2, 512)
        b_, s_, d_ = x.shape
        xf = x.reshape(-1, d_)
        probs = jax.nn.softmax(xf @ router_w + router_b, axis=-1)
        tw, ti = jax.lax.top_k(probs, K)
        tw = tw / jnp.sum(tw, axis=-1, keepdims=True)

        def body(acc, p):
            W1, B1, W2, B2, e = p
            h = jax.nn.silu(xf @ W1 + B1) @ W2 + B2
            cw = jnp.sum(jnp.where(ti == e, tw, 0.0), axis=-1)
            return (acc + cw[:, None] * h, None)
        routed, _ = jax.lax.scan(body, jnp.zeros_like(xf), (w1, b1, w2, b2, jnp.arange(w1.shape[0])))

        def shared_mlp(W1, B1, W2, B2):
            return jax.nn.silu(xf @ W1 + B1) @ W2 + B2
        shared = jnp.sum(jax.vmap(shared_mlp)(sw1, sb1, sw2, sb2), axis=0)
        return (routed + shared).reshape(b_, s_, d_)
    x = x + _L0_xattn_ref(_layernorm(x, axis=-1), ctx_1024, ctx_1024, L0_xattn_Wq, L0_xattn_Wk, L0_xattn_Wv)
    x = x + _L0_ffn_ref(_layernorm(x, axis=-1), L0_ffn_router_w, L0_ffn_router_b, L0_ffn_w1, L0_ffn_b1, L0_ffn_w2, L0_ffn_b2, L0_ffn_sw1, L0_ffn_sb1, L0_ffn_sw2, L0_ffn_sb2)
    return x

_drawn_inputs = setup_inputs


def setup_inputs(seed=0):
    import zlib

    import numpy as np

    out = dict(_drawn_inputs(seed))
    spreads = {'L0_ffn_router_b': (0.0, 2.0),
     'L0_ffn_b1': (0.0, 2.0),
     'L0_ffn_b2': (0.0, 2.0),
     'L0_ffn_sb1': (0.0, 2.0),
     'L0_ffn_sb2': (0.0, 2.0)}
    factors = {'L0_ffn_router_w': 41.954,
     'L0_ffn_w1': 50.583,
     'L0_ffn_w2': 42.507,
     'L0_ffn_sw1': 8.0,
     'L0_ffn_sw2': 8.0}
    for name, (base, spread) in spreads.items():
        noise = np.random.default_rng([zlib.crc32(name.encode()), seed]).standard_normal(out[name].shape)
        drawn = base * np.exp(spread * noise) if base else spread * noise
        out[name] = jnp.asarray(drawn.astype(out[name].dtype))
    for name, factor in factors.items():
        out[name] = (out[name] * factor).astype(out[name].dtype)
    return out
```

```python
from contextlib import ExitStack

import numpy as np

import concourse.bass as bass
from concourse import mybir

F32 = mybir.dt.float32
F32R = mybir.dt.float32r
ALU = mybir.AluOpType
ACT = mybir.ActivationFunctionType
AX_X = mybir.AxisListType.X

P = 128
GAMMA, THETA, SCALE_BASE, EPS = 0.96875, 10000.0, 512.0, 1e-5
TOP = 8


def build(nc, x, ctxT, wqkv, router_w, router_b, w_ffn, b1T, b2, sb2T, ident, rot_q, rot_k, decay, out):
    _, BT, D = x.shape
    B, _, KT, L = ctxT.shape
    E = router_w.shape[2]
    CHUNKS = w_ffn.shape[0]
    TURNS = CHUNKS // 2
    ROUTED = E // 2
    H = P // 2
    LT = L // P
    T = B * L
    HALF = T // 2
    BLK = 512
    NBLK = HALF // BLK
    HT = HALF // P
    assert D == 256 and KT == 2 and L == BLK and NBLK == 2 and BT == B * LT

    cw_dram = nc.dram_tensor("cw_by_expert", [E, T], F32, kind="Internal").ap()

    with ExitStack() as st:
        def sb(name, shape, dt=F32):
            return st.enter_context(nc.sbuf_tensor(name, shape, dt))

        def sem(name):
            return st.enter_context(nc.semaphore(name))

        ps = [st.enter_context(nc.psum_tensor(f"ps{i}", [P, 2, BLK], F32)) for i in range(4)]

        x_sb = sb("x_sb", [P, BT, D])
        xn_hi = sb("xn_hi", [P, KT, T], F32R)
        xn_lo = sb("xn_lo", [P, KT, T], F32R)
        id_sb = sb("id_sb", [P, P])
        cT = sb("cT", [P, 2, KT, L])
        rotq_sb = sb("rotq_sb", [P, 2, L])
        rotk_sb = sb("rotk_sb", [P, 2, L])
        decay_sb = sb("decay_sb", [P, L])
        w_raw = sb("w_raw", [P, 3, KT, D])
        w_hi = sb("w_hi", [P, 3, KT, D], F32R)
        w_lo = sb("w_lo", [P, 3, KT, D], F32R)
        rw_raw = sb("rw_raw", [P, KT, E])
        rw_hi = sb("rw_hi", [P, KT, E], F32R)
        rw_lo = sb("rw_lo", [P, KT, E], F32R)
        rb_sb = sb("rb_sb", [P, E])
        xn = sb("xn", [P, LT, D])
        xn2 = sb("xn2", [P, LT, D])
        xT_hi = sb("xT_hi", [P, KT, L], F32R)
        xT_lo = sb("xT_lo", [P, KT, L], F32R)
        cT_hi = sb("cT_hi", [P, KT, L], F32R)
        cT_lo = sb("cT_lo", [P, KT, L], F32R)
        outT = sb("outT", [P, KT, HALF])
        rot_a = outT[:, 0, :].rearrange("p (s l) -> p s l", l=L)
        rot_b = outT[:, 1, :].rearrange("p (s l) -> p s l", l=L)
        v_hi = sb("v_hi", [P, LT, D], F32R)
        v_lo = sb("v_lo", [P, LT, D], F32R)
        SOFF = [sum(L - P * j for j in range(m)) for m in range(LT + 1)]
        sc = sb("sc", [P, SOFF[LT]])
        sc_hi = sb("sc_hi", [P, SOFF[LT]], F32R)
        sc_lo = sb("sc_lo", [P, SOFF[LT]], F32R)
        stats = sb("stats", [P, 2, LT, 6])
        mv = sb("mv", [P, 2, LT, 2])
        veps = sb("veps", [P, 2, LT])
        rstd = sb("rstd", [P, 2, LT])
        minus_half = sb("minus_half", [P, LT])
        lg = sb("lg", [P, LT, E])
        lmax = sb("lmax", [P, LT])
        lsh = sb("lsh", [P, LT, E])
        ex = sb("ex", [P, LT, E])
        top = sb("top", [P, LT, TOP])
        rest = sb("rest", [P, LT, E])
        sel = sb("sel", [P, LT, E])
        tsum = sb("tsum", [P, LT])
        rsum = sb("rsum", [P, LT])
        cw = sb("cw", [P, LT, E])
        cwT = sb("cwT", [E, T])
        h_hi = sb("h_hi", [P, 2, NBLK, BLK], F32R)
        h_lo = sb("h_lo", [P, 2, NBLK, BLK], F32R)
        h = sb("h", [P, 2, NBLK, BLK])
        cwb = sb("cwb", [P, 2, HALF])
        w1_raw = sb("w1_raw", [P, 2, KT, P])
        w2_raw = sb("w2_raw", [P, 2, D])
        w1_hi = sb("w1_hi", [P, 2, KT, P], F32R)
        w1_lo = sb("w1_lo", [P, 2, KT, P], F32R)
        w2_hi = sb("w2_hi", [P, 2, D], F32R)
        w2_lo = sb("w2_lo", [P, 2, D], F32R)
        b1_sb = sb("b1_sb", [P, CHUNKS])
        sb2_sb = sb("sb2_sb", [P, 2, KT])
        sb2s = sb("sb2s", [P, KT])
        b2_sb = sb("b2_sb", [E, D])

        s_ident, s_rotq, s_rotk, s_decay = sem("s_ident"), sem("s_rotq"), sem("s_rotk"), sem("s_decay")
        s_w, s_rw, s_rb, s_small = sem("s_w"), sem("s_rw"), sem("s_rb"), sem("s_small")
        s_x = [sem(f"s_xin{b}") for b in range(B)]
        s_ctx = [sem(f"s_ctxin{b}") for b in range(B)]
        s_whi, s_wlo, s_rwhi, s_rwlo = sem("s_whi"), sem("s_wlo"), sem("s_rwhi"), sem("s_rwlo")
        s_mh, s_sb2s = sem("s_mh"), sem("s_sb2s")
        s_st1, s_mv1, s_ve1, s_rs1, s_xn = sem("s_st1"), sem("s_mv1"), sem("s_ve1"), sem("s_rs1"), sem("s_xn")
        s_pxT, s_xThi, s_xTlo = sem("s_pxT"), sem("s_xThi"), sem("s_xTlo")
        s_cThi, s_cTlo = sem("s_cThi"), sem("s_cTlo")
        s_pq, s_pk, s_pv = sem("s_pq"), sem("s_pk"), sem("s_pv")
        s_rot = sem("s_rot")
        s_comb = sem("s_comb")
        s_qkhi, s_qklo = sem("s_qkhi"), sem("s_qklo")
        s_vhi, s_vlo = sem("s_vhi"), sem("s_vlo")
        s_ps, s_sc, s_schi, s_sclo = sem("s_ps"), sem("s_sc"), sem("s_schi"), sem("s_sclo")
        s_po, s_x2 = sem("s_po"), sem("s_x2")
        s_st2, s_mv2, s_ve2, s_rs2, s_xn2 = sem("s_st2"), sem("s_mv2"), sem("s_ve2"), sem("s_rs2"), sem("s_xn2")
        s_px2T, s_x2Thi, s_x2Tlo = sem("s_px2T"), sem("s_x2Thi"), sem("s_x2Tlo")
        s_plg, s_lg, s_lmax, s_lsh, s_ex = sem("s_plg"), sem("s_lg"), sem("s_lmax"), sem("s_lsh"), sem("s_ex")
        s_top, s_rest, s_sel, s_tsum, s_rsum, s_cw = (
            sem("s_top"), sem("s_rest"), sem("s_sel"), sem("s_tsum"), sem("s_rsum"), sem("s_cw"))
        s_pcw, s_cwT = sem("s_pcw"), sem("s_cwT")
        s_cwout = [sem(f"s_cwout{b}") for b in range(B)]
        s_w1in = [sem(f"s_w1in{i}") for i in range(2)]
        s_w2in = [sem(f"s_w2in{i}") for i in range(2)]
        s_cwb = [sem(f"s_cwbin{i}") for i in range(2)]
        s_w1hi, s_w1lo, s_w2hi, s_w2lo = sem("s_w1hi"), sem("s_w1lo"), sem("s_w2hi"), sem("s_w2lo")
        s_up, s_silu, s_hcw, s_hhi, s_hlo, s_down = (
            sem("s_up"), sem("s_silu"), sem("s_hcw"), sem("s_hhi"), sem("s_hlo"), sem("s_down"))
        s_outT, s_pout, s_y, s_store = sem("s_outT"), sem("s_pout"), sem("s_y"), sem("s_store")

        def f32(ap):
            return ap.bitcast(F32)

        def three(pe, dst, l_hi, l_lo, r_hi, r_lo, first, last):
            pe.matmul(dst, l_hi, r_lo, start=first, stop=False)
            pe.matmul(dst, l_lo, r_hi, start=False, stop=False)
            return pe.matmul(dst, l_hi, r_hi, start=False, stop=last)

        def over_chunks(eng, half, step):
            step(half, 0, True, False)
            with eng.Fori(1, ROUTED // 2) as i:
                step(half, i, False, False)
            with eng.Fori(ROUTED // 2, TURNS - 1) as i:
                step(half, i, False, True)
            step(half, TURNS - 1, False, True)

        block = st.enter_context(nc.Block())

        @block.sync
        def _(sp):
            sp.dma_start(x_sb[:, 0:LT, :], x[:, 0:LT, :]).then_inc(s_x[0], 16)
            sp.dma_start(id_sb[:], ident).then_inc(s_ident, 16)
            sp.dma_start(cT[:, 0], ctxT[0]).then_inc(s_ctx[0], 16)
            sp.dma_start(w_raw[:], wqkv).then_inc(s_w, 16)
            sp.dma_start(rotq_sb[:], rot_q).then_inc(s_rotq, 16)
            sp.dma_start(rotk_sb[:], rot_k).then_inc(s_rotk, 16)
            sp.dma_start(decay_sb[:], decay).then_inc(s_decay, 16)
            sp.dma_start(x_sb[:, LT:2 * LT, :], x[:, LT:2 * LT, :]).then_inc(s_x[1], 16)
            sp.dma_start(cT[:, 1], ctxT[1]).then_inc(s_ctx[1], 16)
            sp.dma_start(rw_raw[:], router_w).then_inc(s_rw, 16)
            sp.dma_start(rb_sb[:], router_b.partition_broadcast(P)).then_inc(s_rb, 16)
            sp.dma_start(b1_sb[:], b1T).then_inc(s_small, 16)
            sp.dma_start(sb2_sb[:], sb2T).then_inc(s_small, 16)
            sp.dma_start(b2_sb[:], b2).then_inc(s_small, 16)
            for b in range(2, B):
                sp.dma_start(x_sb[:, b * LT:(b + 1) * LT, :], x[:, b * LT:(b + 1) * LT, :]).then_inc(s_x[b], 16)
                sp.wait_ge(s_cTlo, b - 1)
                sp.dma_start(cT[:, b % 2], ctxT[b]).then_inc(s_ctx[b], 16)
            for b in range(B):
                sp.wait_ge(s_cwT, b + 1)
                sp.dma_start(cw_dram[:, b * L:(b + 1) * L], cwT[:, b * L:(b + 1) * L]).then_inc(s_cwout[b], 16)

            def load_w1(c, slot):
                sp.dma_start(w1_raw[:, slot], w_ffn[bass.ds(c, 1), :, 0:KT * P]
                             .rearrange("o p (k h) -> p (o k) h", k=KT)).then_inc(s_w1in[slot], 16)

            def step(half, i, first, shared):
                for slot in range(2):
                    c = i * 2 + slot
                    g = c + half * CHUNKS
                    ahead = (c + 1) % CHUNKS if isinstance(c, int) else c + 1
                    if not (half and isinstance(c, int) and c == CHUNKS - 1):
                        if not (half == 0 and first and slot == 0):
                            sp.wait_ge(s_w1lo, g)
                        load_w1(ahead, 1 - slot)
                    if not (first and half == 0):
                        sp.wait_ge(s_w2lo, g - 1)
                    sp.dma_start(w2_raw[:, slot], w_ffn[bass.ds(c, 1), :, KT * P:]
                                 .rearrange("o p n -> p (o n)")).then_inc(s_w2in[slot], 16)
                    if shared:
                        continue
                    if first and slot == 0:
                        for b in range(half * NBLK, (half + 1) * NBLK):
                            sp.wait_ge(s_cwout[b], 16)
                    if not (first and half == 0):
                        sp.wait_ge(s_hcw, c + half * ROUTED - 1)
                    for e in range(2):
                        sp.dma_start(cwb[e * H:(e + 1) * H, slot, :],
                                     cw_dram[bass.ds(c * 2 + e, 1), half * HALF:(half + 1) * HALF]
                                     .broadcast_to([H, HALF])).then_inc(s_cwb[slot], 16)
            load_w1(0, 0)
            for half in range(2):
                over_chunks(sp, half, step)

        @block.tensor
        def _(pe):
            def transpose_x(b):
                pe.wait_ge(s_xn, b + 1)
                if b >= 1:
                    pe.wait_ge(s_rot, 2 * b - 1)
                for k in range(KT):
                    for t in range(LT):
                        last = pe.transpose(ps[2][:, k, t * P:(t + 1) * P], xn[:, t, k * P:(k + 1) * P], id_sb[:])
                last.then_inc(s_pxT, 1)

            def project(b, which, dst, src_hi, src_lo, done):
                for par in range(2):
                    for k in range(KT):
                        cols = slice(par * P, (par + 1) * P)
                        last = three(pe, dst[:, par, :], w_hi[:, which, k, cols], w_lo[:, which, k, cols],
                                     src_hi[:, k, :], src_lo[:, k, :], k == 0, k == KT - 1)
                last.then_inc(done, 1)

            def project_v(b):
                for t in range(LT):
                    for k in range(KT):
                        rows = slice(t * P, (t + 1) * P)
                        last = three(pe, ps[0][:, t // 2, (t % 2) * D:(t % 2 + 1) * D], cT_hi[:, k, rows],
                                     cT_lo[:, k, rows], w_hi[:, 2, k, :], w_lo[:, 2, k, :], k == 0, k == KT - 1)
                last.then_inc(s_pv, 1)

            def scores(pair, dst):
                for m in (2 * pair, 2 * pair + 1):
                    for par in range(2):
                        n = L - m * P
                        ms = slice(m * P, (m + 1) * P)
                        last = three(pe, dst[:, m % 2, 0:n], h_hi[:, 1, par, ms], h_lo[:, 1, par, ms],
                                     h_hi[:, 0, par, m * P:L], h_lo[:, 0, par, m * P:L], par == 0, par == 1)
                last.then_inc(s_ps, 1)

            def attend(b):
                for t in range(LT):
                    for m in range(t + 1):
                        at = SOFF[m] + (t - m) * P
                        last = three(pe, ps[3][:, t // 2, (t % 2) * D:(t % 2 + 1) * D], sc_hi[:, at:at + P],
                                     sc_lo[:, at:at + P], v_hi[:, m, :], v_lo[:, m, :], m == 0, m == t)
                last.then_inc(s_po, 1)

            def transpose_x2(b):
                pe.wait_ge(s_xn2, b + 1)
                if b >= 1:
                    pe.wait_ge(s_lg, b)
                for k in range(KT):
                    for t in range(LT):
                        last = pe.transpose(ps[1][:, k, t * P:(t + 1) * P], xn2[:, t, k * P:(k + 1) * P], id_sb[:])
                last.then_inc(s_px2T, 1)

            def logits(b):
                pe.wait_ge(s_x2Tlo, b + 1)
                if b == 0:
                    pe.wait_ge(s_rwlo, 1)
                for t in range(LT):
                    rows = slice(b * L + t * P, b * L + (t + 1) * P)
                    for k in range(KT):
                        last = three(pe, ps[1][:, 0, t * E:(t + 1) * E], xn_hi[:, k, rows], xn_lo[:, k, rows],
                                     rw_hi[:, k, :], rw_lo[:, k, :], k == 0, k == KT - 1)
                last.then_inc(s_plg, 1)

            def transpose_cw(b):
                pe.wait_ge(s_cw, b + 1)
                pe.wait_ge(s_sc, min(2 * (b + 2), 2 * B))
                for t in range(LT):
                    last = pe.transpose(ps[0][0:E, 0, t * P:(t + 1) * P], cw[:, t, :], id_sb[:])
                last.then_inc(s_pcw, 1)

            pe.wait_ge(s_ident, 16)
            transpose_x(0)
            for b in range(B):
                pe.wait_ge(s_wlo, 1)
                pe.wait_ge(s_xTlo, b + 1)
                project(b, 0, ps[2], xT_hi, xT_lo, s_pq)
                pe.wait_ge(s_cTlo, b + 1)
                if b >= 1:
                    pe.wait_ge(s_x2, b)
                project(b, 1, ps[3], cT_hi, cT_lo, s_pk)
                if b >= 2:
                    pe.wait_ge(s_cwT, b - 1)
                elif b == 1:
                    pe.wait_ge(s_sc, 2)
                project_v(b)
                if b >= 1:
                    transpose_x2(b - 1)
                if b + 1 < B:
                    transpose_x(b + 1)
                pe.wait_ge(s_qklo, 2 * b + 2)
                scores(0, ps[3])
                if b >= 1:
                    logits(b - 1)
                pe.wait_ge(s_vlo, b + 1)
                scores(1, ps[0])
                pe.wait_ge(s_sclo, 2 * b + 2)
                attend(b)
                if b >= 1:
                    transpose_cw(b - 1)
            transpose_x2(B - 1)
            logits(B - 1)
            transpose_cw(B - 1)

            def up(half, slot):
                for n in range(NBLK):
                    cols = slice(half * HALF + n * BLK, half * HALF + (n + 1) * BLK)
                    for k in range(KT):
                        last = three(pe, ps[slot][:, n, :], w1_hi[:, slot, k, :], w1_lo[:, slot, k, :],
                                     xn_hi[:, k, cols], xn_lo[:, k, cols], k == 0, k == KT - 1)
                last.then_inc(s_up, 1)

            def down(slot, end):
                for k in range(KT):
                    for n in range(NBLK):
                        cols = slice(k * P, (k + 1) * P)
                        last = three(pe, ps[2 + k][:, n, :], w2_hi[:, slot, cols], w2_lo[:, slot, cols],
                                     h_hi[:, slot, n, :], h_lo[:, slot, n, :], False, end)
                last.then_inc(s_down, 1)

            def step(half, i, first, shared):
                for slot in range(2):
                    c = i * 2 + slot
                    g = c + half * CHUNKS
                    pe.wait_ge(s_w1lo, g + 1)
                    if first:
                        if half:
                            pe.wait_ge(s_y, slot + 1)
                    else:
                        pe.wait_ge(s_silu, g - 1)
                    up(half, slot)
                    if first and slot == 0:
                        if half:
                            pe.wait_ge(s_outT, KT)
                        for k in range(KT):
                            for n in range(NBLK):
                                pe.matmul(ps[2 + k][:, n, :], b2_sb[:, k * P:(k + 1) * P],
                                          cwT[:, half * HALF + n * BLK:half * HALF + (n + 1) * BLK],
                                          start=True, stop=False)
                        continue
                    pe.wait_ge(s_w2lo, g)
                    pe.wait_ge(s_hlo, g)
                    down(1 - slot, False)

            pe.wait_ge(s_small, 48)
            pe.wait_ge(s_x2Tlo, B)
            pe.wait_ge(s_cwT, B)
            pe.wait_ge(s_lg, B)
            pe.wait_ge(s_x2, B)
            for half in range(2):
                over_chunks(pe, half, step)
                pe.wait_ge(s_w2lo, (half + 1) * CHUNKS)
                pe.wait_ge(s_hlo, (half + 1) * CHUNKS)
                down(1, True)
                pe.wait_ge(s_silu, (half + 1) * CHUNKS)
                pe.wait_ge(s_outT, (half + 1) * KT)
                for piece in range(2):
                    for t in range(HT // 2):
                        for k in range(KT):
                            at = (piece * HT // 2 + t) * P
                            last = pe.transpose(ps[piece][:, t // 2, (t % 2) * D + k * P:(t % 2) * D + (k + 1) * P],
                                                outT[:, k, at:at + P], id_sb[:])
                    last.then_inc(s_pout, 1)

        @block.scalar
        def _(act):
            act.wait_ge(s_w, 16)
            act.copy(w_hi[:], w_raw[:]).then_inc(s_whi, 1)

            def ctx_hi(b):
                act.wait_ge(s_ctx[b], 16)
                if b >= 1:
                    act.wait_ge(s_pv, b)
                act.copy(cT_hi[:], cT[:, b % 2]).then_inc(s_cThi, 1)

            def x_hi(b):
                act.wait_ge(s_pxT, b + 1)
                if b >= 1:
                    act.wait_ge(s_pq, b)
                act.copy(xT_hi[:], ps[2][:]).then_inc(s_xThi, 1)

            x_hi(0)
            ctx_hi(0)
            act.wait_ge(s_rw, 16)
            act.copy(rw_hi[:], rw_raw[:]).then_inc(s_rwhi, 1)
            for b in range(B):
                act.wait_ge(s_pv, b + 1)
                if b >= 1:
                    act.wait_ge(s_po, b)
                act.copy(v_hi[:], ps[0][:].rearrange("p a (t d) -> p (a t) d", d=D)).then_inc(s_vhi, 1)
                for i in range(2):
                    act.wait_ge(s_comb, 2 * b + i + 1)
                    if b >= 1 and i == 0:
                        act.wait_ge(s_ps, 2 * b)
                    act.copy(h_hi[:, i], h[:, i]).then_inc(s_qkhi, 1)

                def x2_hi(b):
                    act.wait_ge(s_px2T, b + 1)
                    act.copy(xn_hi[:, :, b * L:(b + 1) * L], ps[1][:]).then_inc(s_x2Thi, 1)

                def exps(b):
                    act.wait_ge(s_lsh, b + 1)
                    if b >= 1:
                        act.wait_ge(s_sel, b)
                    act.activation(ex[:], lsh[:], ACT.Exp).then_inc(s_ex, 1)

                if b >= 1:
                    x2_hi(b - 1)
                if b + 1 < B:
                    x_hi(b + 1)
                for i in range(2):
                    act.wait_ge(s_sc, 2 * b + i + 1)
                    if b >= 1 and i == 0:
                        act.wait_ge(s_po, b)
                    part = slice(SOFF[2 * i], SOFF[2 * i + 2])
                    act.copy(sc_hi[:, part], sc[:, part]).then_inc(s_schi, 1)
                    if b >= 1 and i == 0:
                        exps(b - 1)
                if b + 1 < B:
                    ctx_hi(b + 1)
                if b >= 1:
                    act.wait_ge(s_pcw, b)
                    act.copy(cwT[:, (b - 1) * L:b * L], ps[0][0:E, 0, :]).then_inc(s_cwT, 1)
            x2_hi(B - 1)
            exps(B - 1)
            act.wait_ge(s_pcw, B)
            act.copy(cwT[:, (B - 1) * L:B * L], ps[0][0:E, 0, :]).then_inc(s_cwT, 1)

            def w1_split(slot, load):
                act.wait_ge(s_w1in[slot], load * 16)
                act.copy(w1_hi[:, slot], w1_raw[:, slot]).then_inc(s_w1hi, 1)

            def w2_split(slot, load):
                act.wait_ge(s_w2in[slot], load * 16)
                act.copy(w2_hi[:, slot], w2_raw[:, slot]).then_inc(s_w2hi, 1)

            def step(half, i, first, shared):
                for slot in range(2):
                    c = i * 2 + slot
                    g = c + half * CHUNKS
                    act.wait_ge(s_up, g + 1)
                    if first:
                        if half:
                            act.wait_ge(s_hlo, g - 1)
                        else:
                            act.wait_ge(s_qklo, 2 * B)
                    else:
                        act.wait_ge(s_hlo, g - 1)
                    act.activation(h[:, slot], ps[slot][:], ACT.Silu, bias=b1_sb[:, bass.ds(c, 1)]).then_inc(s_silu, 1)
                    turn = i + half * TURNS
                    end = half and isinstance(c, int) and i == TURNS - 1
                    if not end:
                        w1_split(slot, turn + 2)
                    if shared:
                        act.wait_ge(s_silu, g + 1)
                    else:
                        act.wait_ge(s_hcw, c + half * ROUTED + 1)
                    if not (first and half == 0):
                        act.wait_ge(s_down, g - 1)
                    act.copy(h_hi[:, slot], h[:, slot]).then_inc(s_hhi, 1)
                    if not (end and slot):
                        if not (first and half == 0 and slot == 0):
                            act.wait_ge(s_down, g)
                        w2_split(1 - slot, turn + 1 + slot)

            act.wait_ge(s_small, 48)
            w1_split(0, 1)
            w1_split(1, 1)
            w2_split(0, 1)
            for half in range(2):
                over_chunks(act, half, step)
                act.wait_ge(s_down, (half + 1) * CHUNKS)
                act.wait_ge(s_sb2s, 1)
                if half:
                    act.wait_ge(s_pout, 2)
                for k in range(KT):
                    act.activation(outT[:, k, :], ps[2 + k][:].rearrange("p a n -> p (a n)"), ACT.Identity,
                                   bias=sb2s[:, k:k + 1]).then_inc(s_outT, 1)

        @block.vector
        def _(dve):
            def stats_of(b, which, s_st, s_mv):
                for t in range(LT):
                    dve.bn_stats(stats[:, which, t, :], x_sb[:, b * LT + t, :]).then_inc(s_st, 1)
                dve.wait_ge(s_st, LT * (b + 1))
                for t in range(LT):
                    dve.bn_aggr(mv[:, which, t, :], stats[:, which, t, :]).then_inc(s_mv, 1)

            def x_lo(b):
                dve.wait_ge(s_xThi, b + 1)
                dve.tensor_tensor(xT_lo[:], ps[2][:], f32(xT_hi[:]), ALU.subtract).then_inc(s_xTlo, 1)

            def ctx_lo(b):
                dve.wait_ge(s_cThi, b + 1)
                dve.tensor_tensor(cT_lo[:], cT[:, b % 2], f32(cT_hi[:]), ALU.subtract).then_inc(s_cTlo, 1)

            def rotate(b, i, src, table, s_src):
                dve.wait_ge(s_src, b + 1)
                if 2 * b + i >= 1:
                    dve.wait_ge(s_comb, 2 * b + i)
                dve.tensor_tensor(rot_a[:], src[:, 0:1, :].broadcast_to([P, 2, L]), table[:], ALU.mult)
                dve.tensor_tensor(rot_b[:, 0, :], src[:, 1, :], table[:, 1, :], ALU.mult)
                dve.tensor_tensor(rot_b[:, 1, :], src[:, 1, :], table[:, 0, :], ALU.mult).then_inc(s_rot, 1)

            def decayed(b, pair, src):
                dve.wait_ge(s_ps, 2 * b + pair + 1)
                if b >= 1:
                    dve.wait_ge(s_sclo, 2 * b)
                for m in (2 * pair, 2 * pair + 1):
                    n = L - m * P
                    last = dve.tensor_tensor(sc[:, SOFF[m]:SOFF[m + 1]], src[:, m % 2, 0:n], decay_sb[:, 0:n], ALU.mult)
                last.then_inc(s_sc, 1)

            def x2_lo(b):
                dve.wait_ge(s_x2Thi, b + 1)
                cols = slice(b * L, (b + 1) * L)
                dve.tensor_tensor(xn_lo[:, :, cols], ps[1][:], f32(xn_hi[:, :, cols]), ALU.subtract).then_inc(s_x2Tlo, 1)

            def route_1(b):
                dve.wait_ge(s_plg, b + 1)
                dve.tensor_tensor(lg[:], ps[1][:, 0, 0:LT * E].rearrange("p (t e) -> p t e", e=E),
                                  rb_sb[:].unsqueeze(1).broadcast_to([P, LT, E]), ALU.add).then_inc(s_lg, 1)
                dve.wait_ge(s_lg, b + 1)
                dve.tensor_reduce(lmax[:], lg[:], AX_X, ALU.max).then_inc(s_lmax, 1)
                dve.wait_ge(s_lmax, b + 1)
                dve.tensor_tensor(lsh[:], lg[:], lmax[:].unsqueeze(2).broadcast_to([P, LT, E]),
                                  ALU.subtract).then_inc(s_lsh, 1)

            def route_2(b):
                dve.wait_ge(s_ex, b + 1)
                for t in range(LT):
                    dve.max(top[:, t, :], ex[:, t, :]).then_inc(s_top, 1)
                dve.wait_ge(s_top, LT * (b + 1))
                for t in range(LT):
                    dve.match_replace(rest[:, t, :], top[:, t, :], ex[:, t, :], 0.0).then_inc(s_rest, 1)
                dve.tensor_reduce(tsum[:], top[:], AX_X, ALU.add).then_inc(s_tsum, 1)
                dve.wait_ge(s_rest, LT * (b + 1))
                dve.tensor_tensor(sel[:], ex[:], rest[:], ALU.subtract).then_inc(s_sel, 1)
                dve.wait_ge(s_tsum, b + 1)
                dve.reciprocal(rsum[:], tsum[:]).then_inc(s_rsum, 1)
                dve.wait_ge(s_sel, b + 1)
                dve.wait_ge(s_rsum, b + 1)
                if b >= 1:
                    dve.wait_ge(s_pcw, b)
                dve.tensor_tensor(cw[:], sel[:], rsum[:].unsqueeze(2).broadcast_to([P, LT, E]),
                                  ALU.mult).then_inc(s_cw, 1)

            dve.wait_ge(s_x[0], 16)
            stats_of(0, 0, s_st1, s_mv1)
            dve.wait_ge(s_whi, 1)
            dve.tensor_tensor(w_lo[:], w_raw[:], f32(w_hi[:]), ALU.subtract).then_inc(s_wlo, 1)
            x_lo(0)
            ctx_lo(0)
            dve.wait_ge(s_rwhi, 1)
            dve.tensor_tensor(rw_lo[:], rw_raw[:], f32(rw_hi[:]), ALU.subtract).then_inc(s_rwlo, 1)
            dve.wait_ge(s_small, 48)
            dve.tensor_tensor(sb2s[:], sb2_sb[:, 0, :], sb2_sb[:, 1, :], ALU.add).then_inc(s_sb2s, 1)
            dve.wait_ge(s_rotq, 16)
            dve.wait_ge(s_rotk, 16)
            dve.wait_ge(s_decay, 16)
            dve.wait_ge(s_rb, 16)
            for b in range(B):
                rotate(b, 0, ps[2], rotq_sb, s_pq)
                rotate(b, 1, ps[3], rotk_sb, s_pk)
                dve.wait_ge(s_vhi, b + 1)
                dve.tensor_tensor(v_lo[:], ps[0][:].rearrange("p a (t d) -> p (a t) d", d=D), f32(v_hi[:]),
                                  ALU.subtract).then_inc(s_vlo, 1)
                if b >= 1:
                    x2_lo(b - 1)
                if b + 1 < B:
                    dve.wait_ge(s_x[b + 1], 16)
                    dve.wait_ge(s_xn, b + 1)
                    stats_of(b + 1, 0, s_st1, s_mv1)
                decayed(b, 0, ps[3])
                if b + 1 < B:
                    x_lo(b + 1)
                if b >= 1:
                    route_1(b - 1)
                decayed(b, 1, ps[0])
                if b + 1 < B:
                    ctx_lo(b + 1)
                if b >= 1:
                    route_2(b - 1)
                dve.wait_ge(s_po, b + 1)
                rows = x_sb[:, b * LT:(b + 1) * LT, :]
                dve.tensor_tensor(rows, ps[3][:].rearrange("p a (t d) -> p (a t) d", d=D), rows, ALU.add).then_inc(s_x2, 1)
                dve.wait_ge(s_x2, b + 1)
                if b >= 1:
                    dve.wait_ge(s_xn2, b)
                stats_of(b, 1, s_st2, s_mv2)
            x2_lo(B - 1)
            route_1(B - 1)
            route_2(B - 1)

            def w1_rest(slot, count):
                dve.wait_ge(s_w1hi, count)
                dve.tensor_tensor(w1_lo[:, slot], w1_raw[:, slot], f32(w1_hi[:, slot]), ALU.subtract).then_inc(s_w1lo, 1)

            def w2_rest(slot, count):
                dve.wait_ge(s_w2hi, count)
                dve.tensor_tensor(w2_lo[:, slot], w2_raw[:, slot], f32(w2_hi[:, slot]), ALU.subtract).then_inc(s_w2lo, 1)

            def step(half, i, first, shared):
                for slot in range(2):
                    c = i * 2 + slot
                    g = c + half * CHUNKS
                    if not shared:
                        turn = i + half * (ROUTED // 2)
                        dve.wait_ge(s_silu, g + 1)
                        dve.wait_ge(s_cwb[slot], turn * 32 + 32)
                        dve.tensor_tensor(h[:, slot], h[:, slot], cwb[:, slot, :].rearrange("p (a n) -> p a n", n=BLK),
                                          ALU.mult).then_inc(s_hcw, 1)
                    end = half and isinstance(c, int) and i == TURNS - 1
                    if not end:
                        w1_rest(slot, g + 3)
                    dve.wait_ge(s_hhi, g + 1)
                    dve.tensor_tensor(h_lo[:, slot], h[:, slot], f32(h_hi[:, slot]), ALU.subtract).then_inc(s_hlo, 1)
                    if not (end and slot):
                        w2_rest(1 - slot, g + 2)

            w1_rest(0, 1)
            w1_rest(1, 2)
            w2_rest(0, 1)
            for half in range(2):
                over_chunks(dve, half, step)
                for piece in range(2):
                    dve.wait_ge(s_pout, 2 * half + piece + 1)
                    at = half * HT + piece * HT // 2
                    rows = x_sb[:, at:at + HT // 2, :]
                    dve.tensor_tensor(rows, ps[piece][:].rearrange("p a (t d) -> p (a t) d", d=D), rows,
                                      ALU.add).then_inc(s_y, 1)

        @block.gpsimd
        def _(pool):
            pool.memset(minus_half[:], -0.5).then_inc(s_mh, 1)
            pool.wait_ge(s_mh, 1)

            def normalise(b, which, dst, s_mv, s_ve, s_rs, s_done):
                pool.wait_ge(s_mv, LT * (b + 1))
                pool.tensor_scalar(veps[:, which, :], mv[:, which, :, 1], EPS, None, ALU.add).then_inc(s_ve, 1)
                pool.wait_ge(s_ve, b + 1)
                pool.tensor_tensor(rstd[:, which, :], veps[:, which, :], minus_half[:], ALU.pow).then_inc(s_rs, 1)
                pool.wait_ge(s_rs, b + 1)
                for t in range(LT):
                    last = pool.tensor_scalar(dst[:, t, :], x_sb[:, b * LT + t, :], mv[:, which, t, 0:1],
                                              rstd[:, which, t:t + 1], ALU.subtract, ALU.mult)
                last.then_inc(s_done, 1)

            def combine(b, i):
                pool.wait_ge(s_rot, 2 * b + i + 1)
                pool.tensor_tensor(h[:, i, 0, :], rot_a[:, 0, :], rot_b[:, 0, :], ALU.subtract)
                pool.tensor_tensor(h[:, i, 1, :], rot_a[:, 1, :], rot_b[:, 1, :], ALU.add).then_inc(s_comb, 1)
                pool.wait_ge(s_qkhi, 2 * b + i + 1)
                pool.tensor_tensor(h_lo[:, i], h[:, i], f32(h_hi[:, i]), ALU.subtract).then_inc(s_qklo, 1)

            normalise(0, 0, xn, s_mv1, s_ve1, s_rs1, s_xn)
            for b in range(B):
                if b >= 1:
                    normalise(b - 1, 1, xn2, s_mv2, s_ve2, s_rs2, s_xn2)
                combine(b, 0)
                combine(b, 1)
                if b + 1 < B:
                    pool.wait_ge(s_pxT, b + 1)
                    normalise(b + 1, 0, xn, s_mv1, s_ve1, s_rs1, s_xn)
                for i in range(2):
                    pool.wait_ge(s_schi, 2 * b + i + 1)
                    part = slice(SOFF[2 * i], SOFF[2 * i + 2])
                    pool.tensor_tensor(sc_lo[:, part], sc[:, part], f32(sc_hi[:, part]), ALU.subtract).then_inc(s_sclo, 1)
            normalise(B - 1, 1, xn2, s_mv2, s_ve2, s_rs2, s_xn2)

            for n in range(4):
                pool.wait_ge(s_y, n + 1)
                rows = slice(n * HT // 2, (n + 1) * HT // 2)
                pool.dma_start(out[:, rows], x_sb[:, rows]).then_inc(s_store, 16)
            pool.wait_ge(s_store, 4 * 16)


def shape_constants(L, D):
    f = np.float32
    half = D // 2
    scale_vec = (np.arange(0, D, 2, dtype=f) + f(0.4 * D)) / f(1.4 * D)
    pos = np.arange(L, dtype=f)
    scale = scale_vec[None, :] ** (pos / f(SCALE_BASE))[:, None]
    freqs = f(1.0) / f(THETA) ** (np.arange(half, dtype=f) / f(half))
    angle = pos[:, None] * freqs[None, :]
    sin, cos = np.sin(angle), np.cos(angle)
    inverse = f(1.0) / scale
    rot_q = np.stack([(cos * scale).T, (sin * scale).T], axis=1)
    rot_k = np.stack([(cos * inverse).T, (sin * inverse).T], axis=1)
    diff = np.arange(L, dtype=f)[None, :] - np.arange(P, dtype=f)[:, None]
    decay = np.where(diff >= 0, f(GAMMA) ** np.maximum(diff, 0), f(0.0))
    return {"rot_q": rot_q.astype(f), "rot_k": rot_k.astype(f), "decay": decay.astype(f),
            "ident": np.eye(P, dtype=f)}


def laid_out(inputs):
    a = {k: np.asarray(v) for k, v in inputs.items()}
    x, ctx = a["x"], a["ctx_1024"]
    B, L, D = x.shape
    KT, LT = D // P, L // P
    E, _, H = a["L0_ffn_w1"].shape
    ES, _, HS = a["L0_ffn_sw1"].shape
    PAIR, CS = P // H, HS // P

    def rows_by_kt(w):
        return w.reshape(KT, P, w.shape[1]).transpose(1, 0, 2)

    def even_odd(w):
        return np.concatenate([w[:, 0::2], w[:, 1::2]], axis=1)

    wqkv = np.stack([rows_by_kt(even_odd(a["L0_xattn_Wq"])), rows_by_kt(even_odd(a["L0_xattn_Wk"])),
                     rows_by_kt(a["L0_xattn_Wv"])], axis=1)
    w1 = a["L0_ffn_w1"].reshape(E // PAIR, PAIR, KT, P, H).transpose(0, 3, 2, 1, 4).reshape(E // PAIR, P, KT * P)
    sw1 = a["L0_ffn_sw1"].reshape(ES, KT, P, CS, P).transpose(0, 3, 2, 1, 4).reshape(ES * CS, P, KT * P)
    w2 = a["L0_ffn_w2"].reshape(E // PAIR, P, D)
    sw2 = a["L0_ffn_sw2"].reshape(ES * CS, P, D)
    return {
        "x": x.reshape(B * LT, P, D).transpose(1, 0, 2),
        "ctxT": ctx.transpose(0, 2, 1).reshape(B, KT, P, L).transpose(0, 2, 1, 3),
        "wqkv": wqkv,
        "router_w": rows_by_kt(a["L0_ffn_router_w"]),
        "router_b": a["L0_ffn_router_b"],
        "w_ffn": np.concatenate([np.concatenate([w1, w2], axis=2), np.concatenate([sw1, sw2], axis=2)], axis=0),
        "b1T": np.concatenate([a["L0_ffn_b1"].reshape(-1, P), a["L0_ffn_sb1"].reshape(-1, P)], axis=0).T,
        "b2": a["L0_ffn_b2"],
        "sb2T": a["L0_ffn_sb2"].reshape(ES, KT, P).transpose(2, 0, 1),
    }


_NAMES = ["x", "ctxT", "wqkv", "router_w", "router_b", "w_ffn", "b1T", "b2", "sb2T",
          "ident", "rot_q", "rot_k", "decay"]


def kernel(**inputs):
    import concourse.bacc as bacc
    from concourse.bass_utils import run_bass_kernel_spmd

    B, L, D = inputs["x"].shape
    laid = laid_out(inputs)
    laid.update(shape_constants(L, D))
    nc = bacc.Bacc("TRN2", target_bir_lowering=False, num_devices=1)
    arrays, args = {}, []
    for name in _NAMES:
        a = np.ascontiguousarray(laid[name])
        arrays[f"in_{name}"] = a
        args.append(nc.dram_tensor(f"in_{name}", a.shape, mybir.dt.from_np(a.dtype), kind="ExternalInput").ap())
    out = nc.dram_tensor("out_rows", (P, B * L // P, D), F32, kind="ExternalOutput").ap()
    build(nc, *args, out)
    got = run_bass_kernel_spmd(nc, [arrays], core_ids=[0]).results[0]["out_rows"]
    return got.transpose(1, 0, 2).reshape(B, L, D)
```

```python
from contextlib import ExitStack

import numpy as np

import concourse.bass as bass
from concourse import mybir

F32 = mybir.dt.float32
F32R = mybir.dt.float32r
ALU = mybir.AluOpType
ACT = mybir.ActivationFunctionType
AX_X = mybir.AxisListType.X

P = 128
GAMMA, THETA, SCALE_BASE, EPS = 0.96875, 10000.0, 512.0, 1e-5
TOP = 8


def build(nc, x, ctxT, wqkv, router_w, router_b, w_ffn, b1T, b2, sb2T, ident, table_q, table_k, decay, out):
    _, BT, D = x.shape
    B, _, KT, L = ctxT.shape
    E = router_w.shape[2]
    CHUNKS = w_ffn.shape[0]
    TURNS = CHUNKS // 2
    ROUTED = E // 2
    H = P // 2
    LT = L // P
    T = B * L
    HALF = T // 2
    BLK = 512
    NBLK = HALF // BLK
    HT = HALF // P
    assert 2 * E == P and D == 256 and KT == 2 and L == BLK and NBLK == 2 and BT == B * LT

    cw_dram = nc.dram_tensor("cw_by_expert", [E, T], F32, kind="Internal").ap()

    with ExitStack() as st:
        def sb(name, shape, dt=F32):
            return st.enter_context(nc.sbuf_tensor(name, shape, dt))

        def sem(name):
            return st.enter_context(nc.semaphore(name))

        ps = [st.enter_context(nc.psum_tensor(f"ps{i}", [P, 2, BLK], F32)) for i in range(4)]

        x_sb = sb("x_sb", [P, BT, D])
        xn_hi = sb("xn_hi", [P, KT, T], F32R)
        xn_lo = sb("xn_lo", [P, KT, T], F32R)
        id_sb = sb("id_sb", [P, P])
        cT = sb("cT", [P, 2, KT, L])
        tabq_sb = sb("tabq_sb", [P, 2, L])
        tabk_sb = sb("tabk_sb", [P, 2, L])
        decay_sb = sb("decay_sb", [P, L])
        w_raw = sb("w_raw", [P, 3, KT, D])
        w_hi = sb("w_hi", [P, 3, KT, D], F32R)
        w_lo = sb("w_lo", [P, 3, KT, D], F32R)
        rw_raw = sb("rw_raw", [P, KT, E])
        rw_hi = sb("rw_hi", [P, KT, E], F32R)
        rw_lo = sb("rw_lo", [P, KT, E], F32R)
        rb_sb = sb("rb_sb", [P, E])
        xn = sb("xn", [P, LT, D])
        xn2 = sb("xn2", [P, LT, D])
        xT_hi = sb("xT_hi", [P, KT, L], F32R)
        xT_lo = sb("xT_lo", [P, KT, L], F32R)
        cT_hi = sb("cT_hi", [P, KT, L], F32R)
        cT_lo = sb("cT_lo", [P, KT, L], F32R)
        outT = sb("outT", [P, KT, HALF])
        cwb = sb("cwb", [P, 2, HALF])
        rot_q = [outT[:, i, :].rearrange("p (s l) -> p s l", l=L) for i in range(2)]
        rot_k = [cwb[:, i, :].rearrange("p (s l) -> p s l", l=L) for i in range(2)]
        v = sb("v", [P, LT, D])
        SOFF = [sum(L - P * j for j in range(m)) for m in range(LT + 1)]
        sc = sb("sc", [P, SOFF[LT]])
        stats = sb("stats", [P, 2, LT, 6])
        mv = sb("mv", [P, 2, LT, 2])
        veps = sb("veps", [P, 2, LT])
        rstd = sb("rstd", [P, 2, LT])
        scaled_mean = sb("scaled_mean", [P, 2, LT])
        shift = sb("shift", [P, 2, LT])
        minus_half = sb("minus_half", [P, LT])
        lg = sb("lg", [P, LT, E])
        lmax = sb("lmax", [P, LT])
        lsh = sb("lsh", [P, LT, E])
        ex = sb("ex", [P, LT, E])
        top = sb("top", [P, LT, TOP])
        rest = sb("rest", [P, LT, E])
        sel = sb("sel", [P, LT, E])
        tsum = sb("tsum", [P, LT])
        rsum = sb("rsum", [P, LT])
        cw = sb("cw", [P, LT, 2 * E])
        cwT = sb("cwT", [E, L])
        cw_hi = sb("cw_hi", [P, T], F32R)
        cw_lo = sb("cw_lo", [E, T], F32R)
        h_hi = sb("h_hi", [P, 2, NBLK, BLK], F32R)
        h_lo = sb("h_lo", [P, 2, NBLK, BLK], F32R)
        h = sb("h", [P, 2, NBLK, BLK])
        q, k_ = h[:, 0], h[:, 1]
        w1_raw = sb("w1_raw", [P, 2, KT, P])
        w2_raw = sb("w2_raw", [P, 2, D])
        w1_hi = sb("w1_hi", [P, 2, KT, P], F32R)
        w1_lo = sb("w1_lo", [P, 2, KT, P], F32R)
        w2_hi = sb("w2_hi", [P, 2, D], F32R)
        w2_lo = sb("w2_lo", [P, 2, D], F32R)
        b1_sb = sb("b1_sb", [P, NBLK, CHUNKS])
        sb2_sb = sb("sb2_sb", [P, 2, KT])
        sb2s = sb("sb2s", [P, KT])
        b2_raw = sb("b2_raw", [P, D])
        b2_hi = sb("b2_hi", [P, D], F32R)
        b2_hilo = sb("b2_hilo", [P, D], F32R)

        s_ident, s_tabq, s_tabk, s_decay = sem("s_ident"), sem("s_tabq"), sem("s_tabk"), sem("s_decay")
        s_w = [sem(f"s_win{i}") for i in range(3)]
        s_rw, s_rb, s_small = sem("s_rw"), sem("s_rb"), sem("s_small")
        s_x = [sem(f"s_xin{b}") for b in range(B)]
        s_ctx = [sem(f"s_ctxin{b}") for b in range(B)]
        s_whi, s_wlo, s_rwhi, s_rwlo = sem("s_whi"), sem("s_wlo"), sem("s_rwhi"), sem("s_rwlo")
        s_mh, s_sb2s = sem("s_mh"), sem("s_sb2s")
        s_b2hi, s_b2hilo = sem("s_b2hi"), sem("s_b2hilo")
        s_st1, s_mv1, s_ve1, s_rs1, s_sm1, s_sh1, s_xn = (
            sem("s_st1"), sem("s_mv1"), sem("s_ve1"), sem("s_rs1"), sem("s_sm1"), sem("s_sh1"), sem("s_xn"))
        s_pxT, s_xThi, s_xTlo = sem("s_pxT"), sem("s_xThi"), sem("s_xTlo")
        s_cThi, s_cTlo = sem("s_cThi"), sem("s_cTlo")
        s_pq, s_pk, s_pv = sem("s_pq"), sem("s_pk"), sem("s_pv")
        s_rotq, s_rotk, s_q, s_k, s_v = sem("s_rotq"), sem("s_rotk"), sem("s_q"), sem("s_k"), sem("s_v")
        s_ps, s_sc = sem("s_ps"), sem("s_sc")
        s_po, s_x2 = sem("s_po"), sem("s_x2")
        s_st2, s_mv2, s_ve2, s_rs2, s_sm2, s_sh2, s_xn2 = (
            sem("s_st2"), sem("s_mv2"), sem("s_ve2"), sem("s_rs2"), sem("s_sm2"), sem("s_sh2"), sem("s_xn2"))
        s_px2T, s_x2Thi, s_x2Tlo = sem("s_px2T"), sem("s_x2Thi"), sem("s_x2Tlo")
        s_plg, s_lg, s_lmax, s_lsh, s_ex = sem("s_plg"), sem("s_lg"), sem("s_lmax"), sem("s_lsh"), sem("s_ex")
        s_top, s_rest, s_sel, s_tsum, s_rsum, s_cw = (
            sem("s_top"), sem("s_rest"), sem("s_sel"), sem("s_tsum"), sem("s_rsum"), sem("s_cw"))
        s_pcw, s_cwT, s_cwhi, s_cwlo = sem("s_pcw"), sem("s_cwT"), sem("s_cwhi"), sem("s_cwlo")
        s_cwout = [sem(f"s_cwout{b}") for b in range(B)]
        s_w1in = [sem(f"s_w1in{i}") for i in range(2)]
        s_w2in = [sem(f"s_w2in{i}") for i in range(2)]
        s_cwb = [sem(f"s_cwbin{i}") for i in range(2)]
        s_w1hi, s_w1lo, s_w2hi, s_w2lo = sem("s_w1hi"), sem("s_w1lo"), sem("s_w2hi"), sem("s_w2lo")
        s_up, s_silu, s_hcw, s_hhi, s_hlo, s_down = (
            sem("s_up"), sem("s_silu"), sem("s_hcw"), sem("s_hhi"), sem("s_hlo"), sem("s_down"))
        s_outT, s_pout, s_y, s_store = sem("s_outT"), sem("s_pout"), sem("s_y"), sem("s_store")

        def f32(ap):
            return ap.bitcast(F32)

        def three(pe, dst, l_hi, l_lo, r_hi, r_lo, first, last):
            pe.matmul(dst, l_hi, r_lo, start=first, stop=False)
            pe.matmul(dst, l_lo, r_hi, start=False, stop=False)
            return pe.matmul(dst, l_hi, r_hi, start=False, stop=last)

        def score_ps(m):
            n = L - m * P
            return ps[0][:, m, 0:n] if m < 2 else ps[1][:, 0, (m - 2) * 2 * P:(m - 2) * 2 * P + n]

        def over_chunks(eng, half, step):
            step(half, 0, True, False)
            with eng.Fori(1, ROUTED // 2) as i:
                step(half, i, False, False)
            with eng.Fori(ROUTED // 2, TURNS - 1) as i:
                step(half, i, False, True)
            step(half, TURNS - 1, False, True)

        block = st.enter_context(nc.Block())

        @block.sync
        def _(sp):
            def load_x(b):
                sp.dma_start(x_sb[:, b * LT:(b + 1) * LT, :], x[:, b * LT:(b + 1) * LT, :]).then_inc(s_x[b], 16)

            def load_w(i):
                sp.dma_start(w_raw[:, i], wqkv[:, i]).then_inc(s_w[i], 16)

            load_w(1)
            sp.dma_start(cT[:, 0], ctxT[0]).then_inc(s_ctx[0], 16)
            load_x(0)
            load_w(2)
            sp.dma_start(id_sb[:], ident).then_inc(s_ident, 16)
            sp.dma_start(tabk_sb[:], table_k).then_inc(s_tabk, 16)
            load_w(0)
            sp.dma_start(tabq_sb[:], table_q).then_inc(s_tabq, 16)
            load_x(1)
            sp.dma_start(cT[:, 1], ctxT[1]).then_inc(s_ctx[1], 16)
            sp.dma_start(decay_sb[:], decay).then_inc(s_decay, 16)
            sp.dma_start(rw_raw[:], router_w).then_inc(s_rw, 16)
            sp.dma_start(rb_sb[:], router_b.partition_broadcast(P)).then_inc(s_rb, 16)
            for i in range(NBLK):
                sp.dma_start(b1_sb[:, i], b1T).then_inc(s_small, 16)
            sp.dma_start(sb2_sb[:], sb2T).then_inc(s_small, 16)
            for i in range(2):
                sp.dma_start(b2_raw[i * E:(i + 1) * E, :], b2).then_inc(s_small, 16)
            for b in range(2, B):
                load_x(b)
                sp.wait_ge(s_cTlo, b - 1)
                sp.dma_start(cT[:, b % 2], ctxT[b]).then_inc(s_ctx[b], 16)

            def load_w1(c, slot):
                sp.dma_start(w1_raw[:, slot], w_ffn[bass.ds(c, 1), :, 0:KT * P]
                             .rearrange("o p (k h) -> p (o k) h", k=KT)).then_inc(s_w1in[slot], 16)

            def step(half, i, first, shared):
                for slot in range(2):
                    c = i * 2 + slot
                    g = c + half * CHUNKS
                    ahead = (c + 1) % CHUNKS if isinstance(c, int) else c + 1
                    if not (half and isinstance(c, int) and c == CHUNKS - 1):
                        if not (half == 0 and first and slot == 0):
                            sp.wait_ge(s_w1lo, g)
                        load_w1(ahead, 1 - slot)
                    if not (first and half == 0):
                        sp.wait_ge(s_w2lo, g - 1)
                    sp.dma_start(w2_raw[:, slot], w_ffn[bass.ds(c, 1), :, KT * P:]
                                 .rearrange("o p n -> p (o n)")).then_inc(s_w2in[slot], 16)
                    if shared:
                        continue
                    if first and slot == 0:
                        for b in range(half * NBLK, (half + 1) * NBLK):
                            sp.wait_ge(s_cwout[b], 16)
                        if half == 0:
                            sp.wait_ge(s_k, B)
                    if not (first and half == 0):
                        sp.wait_ge(s_hcw, NBLK * (c + half * ROUTED - 1))
                    for e in range(2):
                        sp.dma_start(cwb[e * H:(e + 1) * H, slot, :],
                                     cw_dram[bass.ds(c * 2 + e, 1), half * HALF:(half + 1) * HALF]
                                     .broadcast_to([H, HALF])).then_inc(s_cwb[slot], 16)
            load_w1(0, 0)
            for half in range(2):
                over_chunks(sp, half, step)

        @block.tensor
        def _(pe):
            def transpose_x(b, dst):
                pe.wait_ge(s_xn, b + 1)
                for k in range(KT):
                    for t in range(LT):
                        last = pe.transpose(dst[:, k, t * P:(t + 1) * P], xn[:, t, k * P:(k + 1) * P], id_sb[:])
                last.then_inc(s_pxT, 1)

            def project(which, dst, src_hi, src_lo, done):
                for par in range(2):
                    for k in range(KT):
                        cols = slice(par * P, (par + 1) * P)
                        last = three(pe, dst[:, par, :], w_hi[:, which, k, cols], w_lo[:, which, k, cols],
                                     src_hi[:, k, :], src_lo[:, k, :], k == 0, k == KT - 1)
                last.then_inc(done, 1)

            def project_q(b):
                pe.wait_ge(s_xTlo, b + 1)
                if b >= 1:
                    pe.wait_ge(s_sc, 2 * b - 1)
                project(0, ps[0], xT_hi, xT_lo, s_pq)

            def project_k(b):
                pe.wait_ge(s_cTlo, b + 1)
                if b >= 1:
                    pe.wait_ge(s_sc, 2 * b)
                if b >= 3:
                    pe.wait_ge(s_cwlo, b - 2)
                project(1, ps[1], cT_hi, cT_lo, s_pk)

            def project_v(b):
                if b >= 1:
                    pe.wait_ge(s_x2, b)
                for t in range(LT):
                    for k in range(KT):
                        rows = slice(t * P, (t + 1) * P)
                        last = three(pe, ps[3][:, t // 2, (t % 2) * D:(t % 2 + 1) * D], cT_hi[:, k, rows],
                                     cT_lo[:, k, rows], w_hi[:, 2, k, :], w_lo[:, 2, k, :], k == 0, k == KT - 1)
                last.then_inc(s_pv, 1)

            def scores(b, pair):
                for m in (2 * pair, 2 * pair + 1):
                    for par in range(2):
                        last = pe.matmul(score_ps(m), k_[:, par, m * P:(m + 1) * P], q[:, par, m * P:L],
                                         start=par == 0, stop=par == 1)
                last.then_inc(s_ps, 1)

            def attend(b):
                pe.wait_ge(s_sc, 2 * b + 2)
                pe.wait_ge(s_v, b + 1)
                for t in range(LT):
                    for m in range(t + 1):
                        at = SOFF[m] + (t - m) * P
                        last = pe.matmul(ps[3][:, t // 2, (t % 2) * D:(t % 2 + 1) * D], sc[:, at:at + P],
                                         v[:, m, :], start=m == 0, stop=m == t)
                last.then_inc(s_po, 1)

            def transpose_x2(b):
                pe.wait_ge(s_xn2, b + 1)
                if b >= 1:
                    pe.wait_ge(s_lg, b)
                for k in range(KT):
                    for t in range(LT):
                        last = pe.transpose(ps[2][:, k, t * P:(t + 1) * P], xn2[:, t, k * P:(k + 1) * P], id_sb[:])
                last.then_inc(s_px2T, 1)

            def logits(b):
                pe.wait_ge(s_x2Tlo, b + 1)
                if b == 0:
                    pe.wait_ge(s_rwlo, 1)
                for t in range(LT):
                    rows = slice(b * L + t * P, b * L + (t + 1) * P)
                    for k in range(KT):
                        last = three(pe, ps[2][:, 0, t * E:(t + 1) * E], xn_hi[:, k, rows], xn_lo[:, k, rows],
                                     rw_hi[:, k, :], rw_lo[:, k, :], k == 0, k == KT - 1)
                last.then_inc(s_plg, 1)

            def transpose_cw(b, dst):
                pe.wait_ge(s_cw, b + 1)
                for t in range(LT):
                    last = pe.transpose(dst[:, t * P:(t + 1) * P], cw[:, t], id_sb[:])
                last.then_inc(s_pcw, 1)

            pe.wait_ge(s_wlo, 1)
            project_k(0)
            pe.wait_ge(s_wlo, 2)
            project_v(0)
            pe.wait_ge(s_ident, 16)
            transpose_x(0, ps[2])
            pe.wait_ge(s_wlo, 3)
            project_q(0)
            pe.wait_ge(s_rotq, 1)
            transpose_x(1, ps[0])
            for b in range(B):
                pe.wait_ge(s_q, b + 1)
                pe.wait_ge(s_k, b + 1)
                pe.wait_ge(s_xTlo, min(b + 2, B))
                scores(b, 0)
                scores(b, 1)
                if b >= 2:
                    transpose_cw(b - 2, ps[1][:, 1, :])
                if b >= 1:
                    transpose_x2(b - 1)
                if b + 1 < B:
                    project_q(b + 1)
                    project_k(b + 1)
                attend(b)
                if b >= 1:
                    logits(b - 1)
                if b + 1 < B:
                    project_v(b + 1)
                if b + 2 < B:
                    pe.wait_ge(s_rotq, b + 2)
                    transpose_x(b + 2, ps[0])

            def up(half, slot):
                for n in range(NBLK):
                    cols = slice(half * HALF + n * BLK, half * HALF + (n + 1) * BLK)
                    for k in range(KT):
                        last = three(pe, ps[slot][:, n, :], w1_hi[:, slot, k, :], w1_lo[:, slot, k, :],
                                     xn_hi[:, k, cols], xn_lo[:, k, cols], k == 0, k == KT - 1)
                    last.then_inc(s_up, 1)

            def down(slot, g, end):
                pe.wait_ge(s_w2lo, g + 1)
                for n in range(NBLK):
                    pe.wait_ge(s_hlo, NBLK * g + n + 1)
                    for k in range(KT):
                        cols = slice(k * P, (k + 1) * P)
                        last = three(pe, ps[2 + k][:, n, :], w2_hi[:, slot, cols], w2_lo[:, slot, cols],
                                     h_hi[:, slot, n, :], h_lo[:, slot, n, :], False, end)
                last.then_inc(s_down, 1)

            def step(half, i, first, shared):
                for slot in range(2):
                    c = i * 2 + slot
                    g = c + half * CHUNKS
                    pe.wait_ge(s_w1lo, g + 1)
                    if first:
                        if half:
                            pe.wait_ge(s_y, slot + 1)
                    else:
                        pe.wait_ge(s_silu, NBLK * (g - 1))
                    up(half, slot)
                    if first and slot == 0:
                        if half == 0:
                            transpose_x2(B - 1)
                            pe.wait_ge(s_x2, B)
                            transpose_cw(B - 2, ps[3][:, 0, :])
                        continue
                    if first:
                        if half:
                            pe.wait_ge(s_outT, KT)
                        else:
                            logits(B - 1)
                            pe.wait_ge(s_lg, B)
                            pe.wait_ge(s_cwlo, B - 1)
                            pe.wait_ge(s_b2hilo, 2)
                        for k in range(KT):
                            for n in range(NBLK):
                                rows = slice(half * HALF + n * BLK, half * HALF + (n + 1) * BLK)
                                dst, cols = ps[2 + k][:, n, :], slice(k * P, (k + 1) * P)
                                pe.matmul(dst, b2_hilo[:, cols], cw_hi[:, rows], start=True, stop=False)
                                pe.matmul(dst, b2_hilo[0:E, cols], cw_lo[:, rows], start=False, stop=False)
                    down(1 - slot, g - 1, False)
                    if first and half == 0:
                        pe.wait_ge(s_silu, NBLK)
                        transpose_cw(B - 1, ps[0][:, 0, :])
                        pe.wait_ge(s_cwlo, B)

            for half in range(2):
                over_chunks(pe, half, step)
                down(1, (half + 1) * CHUNKS - 1, True)
                pe.wait_ge(s_silu, NBLK * (half + 1) * CHUNKS)
                pe.wait_ge(s_outT, (half + 1) * KT)
                for piece in range(2):
                    for t in range(HT // 2):
                        for k in range(KT):
                            at = (piece * HT // 2 + t) * P
                            last = pe.transpose(ps[piece][:, t // 2, (t % 2) * D + k * P:(t % 2) * D + (k + 1) * P],
                                                outT[:, k, at:at + P], id_sb[:])
                    last.then_inc(s_pout, 1)

        @block.scalar
        def _(act):
            def w_split(i):
                act.wait_ge(s_w[i], 16)
                act.copy(w_hi[:, i], w_raw[:, i]).then_inc(s_whi, 1)

            def ctx_hi(b):
                act.wait_ge(s_ctx[b], 16)
                if b >= 1:
                    act.wait_ge(s_pv, b)
                act.copy(cT_hi[:], cT[:, b % 2]).then_inc(s_cThi, 1)

            def x_hi(b, src):
                act.wait_ge(s_pxT, b + 1)
                if b >= 1:
                    act.wait_ge(s_pq, b)
                act.copy(xT_hi[:], src[:]).then_inc(s_xThi, 1)

            def normalise(b, which, dst, s_shift, s_used, s_done):
                act.wait_ge(s_shift, b + 1)
                if b >= 1:
                    act.wait_ge(s_used, b)
                for t in range(LT):
                    last = act.activation(dst[:, t, :], x_sb[:, b * LT + t, :], ACT.Identity,
                                          bias=shift[:, which, t:t + 1], scale=rstd[:, which, t:t + 1])
                last.then_inc(s_done, 1)

            def v_copy(b):
                act.wait_ge(s_pv, b + 1)
                if b >= 1:
                    act.wait_ge(s_po, b)
                act.copy(v[:], ps[3][:].rearrange("p a (t d) -> p (a t) d", d=D)).then_inc(s_v, 1)

            def x2_hi(b):
                act.wait_ge(s_px2T, b + 1)
                act.copy(xn_hi[:, :, b * L:(b + 1) * L], ps[2][:]).then_inc(s_x2Thi, 1)

            def exps(b):
                act.wait_ge(s_lsh, b + 1)
                if b >= 1:
                    act.wait_ge(s_sel, b)
                act.activation(ex[:], lsh[:], ACT.Exp).then_inc(s_ex, 1)

            def cw_copy(b, src):
                act.wait_ge(s_pcw, b + 1)
                if b >= 1:
                    act.wait_ge(s_cwout[b - 1], 16)
                act.copy(cwT[:], src[0:E, :]).then_inc(s_cwT, 1)
                act.copy(cw_hi[:, b * L:(b + 1) * L], src).then_inc(s_cwhi, 1)

            w_split(1)
            ctx_hi(0)
            w_split(2)
            normalise(0, 0, xn, s_sh1, s_pxT, s_xn)
            w_split(0)
            v_copy(0)
            x_hi(0, ps[2])
            normalise(1, 0, xn, s_sh1, s_pxT, s_xn)
            ctx_hi(1)
            x_hi(1, ps[0])
            act.wait_ge(s_rw, 16)
            act.copy(rw_hi[:], rw_raw[:]).then_inc(s_rwhi, 1)
            act.wait_ge(s_small, 80)
            act.copy(b2_hi[:], b2_raw[:]).then_inc(s_b2hi, 1)
            act.copy(b2_hilo[0:E], b2_raw[0:E]).then_inc(s_b2hilo, 1)
            for b in range(B):
                if b + 2 < B:
                    normalise(b + 2, 0, xn, s_sh1, s_pxT, s_xn)
                if b >= 2:
                    cw_copy(b - 2, ps[1][:, 1, :])
                if b >= 1:
                    x2_hi(b - 1)
                    exps(b - 1)
                if b + 1 < B:
                    v_copy(b + 1)
                if b + 2 < B:
                    x_hi(b + 2, ps[0])
                    ctx_hi(b + 2)
                normalise(b, 1, xn2, s_sh2, s_px2T, s_xn2)

            def w1_split(slot, load):
                act.wait_ge(s_w1in[slot], load * 16)
                act.copy(w1_hi[:, slot], w1_raw[:, slot]).then_inc(s_w1hi, 1)

            def w2_split(slot, load):
                act.wait_ge(s_w2in[slot], load * 16)
                act.copy(w2_hi[:, slot], w2_raw[:, slot]).then_inc(s_w2hi, 1)

            def step(half, i, first, shared):
                for slot in range(2):
                    c = i * 2 + slot
                    g = c + half * CHUNKS
                    turn = i + half * TURNS
                    end = half and isinstance(c, int) and i == TURNS - 1
                    for n in range(NBLK):
                        act.wait_ge(s_up, NBLK * g + n + 1)
                        if first and half == 0:
                            act.wait_ge(s_ps, 2 * B)
                        else:
                            act.wait_ge(s_hlo, NBLK * (g - 2) + n + 1)
                        act.activation(h[:, slot, n], ps[slot][:, n, :], ACT.Silu,
                                       bias=b1_sb[:, n, bass.ds(c, 1)]).then_inc(s_silu, 1)
                    if not end:
                        w1_split(slot, turn + 2)
                    if first and half == 0 and slot == 0:
                        x2_hi(B - 1)
                        cw_copy(B - 2, ps[3][:, 0, :])
                    for n in range(NBLK):
                        if shared:
                            act.wait_ge(s_silu, NBLK * g + n + 1)
                        else:
                            act.wait_ge(s_hcw, NBLK * (c + half * ROUTED) + n + 1)
                        if not (first and half == 0):
                            act.wait_ge(s_down, g - 1)
                        act.copy(h_hi[:, slot, n], h[:, slot, n]).then_inc(s_hhi, 1)
                    if first and half == 0 and slot:
                        exps(B - 1)
                    if not (end and slot):
                        if not (first and half == 0 and slot == 0):
                            act.wait_ge(s_down, g)
                        w2_split(1 - slot, turn + 1 + slot)
                    if first and half == 0 and slot:
                        cw_copy(B - 1, ps[0][:, 0, :])
                        act.preload_act_table(ACT.Silu)

            w1_split(0, 1)
            w1_split(1, 1)
            w2_split(0, 1)
            for half in range(2):
                over_chunks(act, half, step)
                act.wait_ge(s_down, (half + 1) * CHUNKS)
                act.wait_ge(s_sb2s, 1)
                if half:
                    act.wait_ge(s_pout, 2)
                for k in range(KT):
                    act.activation(outT[:, k, :], ps[2 + k][:].rearrange("p a n -> p (a n)"), ACT.Identity,
                                   bias=sb2s[:, k:k + 1]).then_inc(s_outT, 1)

        @block.vector
        def _(dve):
            def stats_of(b, which, s_st, s_mv, s_shift):
                if b >= 1:
                    dve.wait_ge(s_shift, b)
                for t in range(LT):
                    dve.bn_stats(stats[:, which, t, :], x_sb[:, b * LT + t, :]).then_inc(s_st, 1)
                dve.wait_ge(s_st, LT * (b + 1))
                for t in range(LT):
                    dve.bn_aggr(mv[:, which, t, :], stats[:, which, t, :]).then_inc(s_mv, 1)

            def w_rest(i, count):
                dve.wait_ge(s_whi, count)
                dve.tensor_tensor(w_lo[:, i], w_raw[:, i], f32(w_hi[:, i]), ALU.subtract).then_inc(s_wlo, 1)

            def x_lo(b, src):
                dve.wait_ge(s_xThi, b + 1)
                dve.tensor_tensor(xT_lo[:], src[:], f32(xT_hi[:]), ALU.subtract).then_inc(s_xTlo, 1)

            def rotate(b, src, table, rot, s_src, s_used, s_done):
                dve.wait_ge(s_src, b + 1)
                if b >= 1:
                    dve.wait_ge(s_used, b)
                for par in range(2):
                    last = dve.tensor_tensor(rot[par], src[:, par:par + 1, :].broadcast_to([P, 2, L]), table[:],
                                             ALU.mult)
                last.then_inc(s_done, 1)

            def decayed(b, pair):
                dve.wait_ge(s_ps, 2 * b + pair + 1)
                if b >= 1:
                    dve.wait_ge(s_po, b)
                for m in (2 * pair, 2 * pair + 1):
                    last = dve.tensor_tensor(sc[:, SOFF[m]:SOFF[m + 1]], score_ps(m), decay_sb[:, 0:L - m * P], ALU.mult)
                last.then_inc(s_sc, 1)

            def x2_lo(b):
                dve.wait_ge(s_x2Thi, b + 1)
                cols = slice(b * L, (b + 1) * L)
                dve.tensor_tensor(xn_lo[:, :, cols], ps[2][:], f32(xn_hi[:, :, cols]), ALU.subtract).then_inc(s_x2Tlo, 1)

            def route_1(b):
                dve.wait_ge(s_plg, b + 1)
                dve.tensor_tensor(lg[:], ps[2][:, 0, 0:LT * E].rearrange("p (t e) -> p t e", e=E),
                                  rb_sb[:].unsqueeze(1).broadcast_to([P, LT, E]), ALU.add).then_inc(s_lg, 1)
                dve.wait_ge(s_lg, b + 1)
                dve.tensor_reduce(lmax[:], lg[:], AX_X, ALU.max).then_inc(s_lmax, 1)
                dve.wait_ge(s_lmax, b + 1)
                dve.tensor_tensor(lsh[:], lg[:], lmax[:].unsqueeze(2).broadcast_to([P, LT, E]),
                                  ALU.subtract).then_inc(s_lsh, 1)

            def route_2(b):
                dve.wait_ge(s_ex, b + 1)
                for t in range(LT):
                    dve.max(top[:, t, :], ex[:, t, :]).then_inc(s_top, 1)
                dve.wait_ge(s_top, LT * (b + 1))
                for t in range(LT):
                    dve.match_replace(rest[:, t, :], top[:, t, :], ex[:, t, :], 0.0).then_inc(s_rest, 1)
                dve.tensor_reduce(tsum[:], top[:], AX_X, ALU.add).then_inc(s_tsum, 1)
                dve.wait_ge(s_rest, LT * (b + 1))
                dve.tensor_tensor(sel[:], ex[:], rest[:], ALU.subtract).then_inc(s_sel, 1)
                dve.wait_ge(s_tsum, b + 1)
                dve.reciprocal(rsum[:], tsum[:]).then_inc(s_rsum, 1)
                dve.wait_ge(s_sel, b + 1)
                dve.wait_ge(s_rsum, b + 1)
                if b >= 1:
                    dve.wait_ge(s_pcw, b)
                for i in range(2):
                    last = dve.tensor_tensor(cw[:, :, i * E:(i + 1) * E], sel[:],
                                             rsum[:].unsqueeze(2).broadcast_to([P, LT, E]), ALU.mult)
                last.then_inc(s_cw, 1)

            def cw_rest(b, src):
                dve.wait_ge(s_cwhi, b + 1)
                cols = slice(b * L, (b + 1) * L)
                dve.tensor_tensor(cw_lo[:, cols], src[0:E, :], f32(cw_hi[0:E, cols]), ALU.subtract).then_inc(s_cwlo, 1)

            def attended(b):
                dve.wait_ge(s_po, b + 1)
                rows = x_sb[:, b * LT:(b + 1) * LT, :]
                dve.tensor_tensor(rows, ps[3][:].rearrange("p a (t d) -> p (a t) d", d=D), rows, ALU.add).then_inc(s_x2, 1)

            def attended_stats(b):
                dve.wait_ge(s_x2, b + 1)
                stats_of(b, 1, s_st2, s_mv2, s_sh2)

            def combine_q(b):
                dve.wait_ge(s_rotq, b + 1)
                if b >= 1:
                    dve.wait_ge(s_ps, 2 * b)
                dve.tensor_tensor(q[:, 0, :], rot_q[0][:, 0, :], rot_q[1][:, 1, :], ALU.subtract)
                dve.tensor_tensor(q[:, 1, :], rot_q[0][:, 1, :], rot_q[1][:, 0, :], ALU.add).then_inc(s_q, 1)

            w_rest(1, 1)
            dve.wait_ge(s_cThi, 1)
            dve.tensor_tensor(cT_lo[:], cT[:, 0], f32(cT_hi[:]), ALU.subtract).then_inc(s_cTlo, 1)
            dve.wait_ge(s_x[0], 16)
            stats_of(0, 0, s_st1, s_mv1, s_sh1)
            w_rest(2, 2)
            dve.wait_ge(s_tabk, 16)
            dve.wait_ge(s_x[1], 16)
            stats_of(1, 0, s_st1, s_mv1, s_sh1)
            rotate(0, ps[1], tabk_sb, rot_k, s_pk, s_k, s_rotk)
            w_rest(0, 3)
            x_lo(0, ps[2])
            dve.wait_ge(s_tabq, 16)
            rotate(0, ps[0], tabq_sb, rot_q, s_pq, s_q, s_rotq)
            combine_q(0)
            x_lo(1, ps[0])
            dve.wait_ge(s_rwhi, 1)
            dve.tensor_tensor(rw_lo[:], rw_raw[:], f32(rw_hi[:]), ALU.subtract).then_inc(s_rwlo, 1)
            dve.wait_ge(s_small, 80)
            dve.tensor_tensor(sb2s[:], sb2_sb[:, 0, :], sb2_sb[:, 1, :], ALU.add).then_inc(s_sb2s, 1)
            dve.wait_ge(s_b2hi, 1)
            dve.tensor_tensor(b2_hilo[E:2 * E], b2_raw[E:2 * E], f32(b2_hi[E:2 * E]), ALU.subtract).then_inc(s_b2hilo, 1)
            dve.wait_ge(s_decay, 16)
            dve.wait_ge(s_rb, 16)
            for b in range(B):
                if b + 2 < B:
                    dve.wait_ge(s_x[b + 2], 16)
                    stats_of(b + 2, 0, s_st1, s_mv1, s_sh1)
                decayed(b, 0)
                decayed(b, 1)
                if b >= 2:
                    cw_rest(b - 2, ps[1][:, 1, :])
                if b >= 1:
                    x2_lo(b - 1)
                if b + 1 < B:
                    rotate(b + 1, ps[0], tabq_sb, rot_q, s_pq, s_q, s_rotq)
                    combine_q(b + 1)
                    rotate(b + 1, ps[1], tabk_sb, rot_k, s_pk, s_k, s_rotk)
                attended(b)
                if b >= 1:
                    route_1(b - 1)
                attended_stats(b)
                if b + 2 < B:
                    x_lo(b + 2, ps[0])
                if b >= 1:
                    route_2(b - 1)

            def w1_rest(slot, count):
                dve.wait_ge(s_w1hi, count)
                dve.tensor_tensor(w1_lo[:, slot], w1_raw[:, slot], f32(w1_hi[:, slot]), ALU.subtract).then_inc(s_w1lo, 1)

            def w2_rest(slot, count):
                dve.wait_ge(s_w2hi, count)
                dve.tensor_tensor(w2_lo[:, slot], w2_raw[:, slot], f32(w2_hi[:, slot]), ALU.subtract).then_inc(s_w2lo, 1)

            def step(half, i, first, shared):
                for slot in range(2):
                    c = i * 2 + slot
                    g = c + half * CHUNKS
                    end = half and isinstance(c, int) and i == TURNS - 1
                    if not shared:
                        turn = i + half * (ROUTED // 2)
                        dve.wait_ge(s_cwb[slot], turn * 32 + 32)
                        for n in range(NBLK):
                            dve.wait_ge(s_silu, NBLK * g + n + 1)
                            dve.tensor_tensor(h[:, slot, n], h[:, slot, n], cwb[:, slot, n * BLK:(n + 1) * BLK],
                                              ALU.mult).then_inc(s_hcw, 1)
                    if not end:
                        w1_rest(slot, g + 3)
                    if first and half == 0 and slot == 0:
                        x2_lo(B - 1)
                        cw_rest(B - 2, ps[3][:, 0, :])
                    for n in range(NBLK):
                        dve.wait_ge(s_hhi, NBLK * g + n + 1)
                        dve.tensor_tensor(h_lo[:, slot, n], h[:, slot, n], f32(h_hi[:, slot, n]),
                                          ALU.subtract).then_inc(s_hlo, 1)
                    if first and half == 0 and slot:
                        route_1(B - 1)
                    if not (end and slot):
                        w2_rest(1 - slot, g + 2)
                    if first and half == 0 and slot:
                        route_2(B - 1)
                        cw_rest(B - 1, ps[0][:, 0, :])

            w1_rest(0, 1)
            w1_rest(1, 2)
            w2_rest(0, 1)
            for half in range(2):
                over_chunks(dve, half, step)
                for piece in range(2):
                    dve.wait_ge(s_pout, 2 * half + piece + 1)
                    at = half * HT + piece * HT // 2
                    rows = x_sb[:, at:at + HT // 2, :]
                    dve.tensor_tensor(rows, ps[piece][:].rearrange("p a (t d) -> p (a t) d", d=D), rows,
                                      ALU.add).then_inc(s_y, 1)

        @block.gpsimd
        def _(pool):
            pool.memset(minus_half[:], -0.5).then_inc(s_mh, 1)
            pool.wait_ge(s_mh, 1)

            def scale_shift(b, which, s_mv, s_used, s_ve, s_rs, s_sm, s_shift):
                pool.wait_ge(s_mv, LT * (b + 1))
                if b >= 1:
                    pool.wait_ge(s_used, b)
                pool.tensor_scalar(veps[:, which, :], mv[:, which, :, 1], EPS, None, ALU.add).then_inc(s_ve, 1)
                pool.wait_ge(s_ve, b + 1)
                pool.tensor_tensor(rstd[:, which, :], veps[:, which, :], minus_half[:], ALU.pow).then_inc(s_rs, 1)
                pool.wait_ge(s_rs, b + 1)
                pool.tensor_tensor(scaled_mean[:, which, :], mv[:, which, :, 0], rstd[:, which, :], ALU.mult).then_inc(s_sm, 1)
                pool.wait_ge(s_sm, b + 1)
                pool.tensor_scalar(shift[:, which, :], scaled_mean[:, which, :], -1.0, None, ALU.mult).then_inc(s_shift, 1)

            def combine_k(b):
                pool.wait_ge(s_rotk, b + 1)
                if b >= 1:
                    pool.wait_ge(s_ps, 2 * b)
                pool.tensor_tensor(k_[:, 0, :], rot_k[0][:, 0, :], rot_k[1][:, 1, :], ALU.subtract)
                pool.tensor_tensor(k_[:, 1, :], rot_k[0][:, 1, :], rot_k[1][:, 0, :], ALU.add).then_inc(s_k, 1)

            def ctx_lo(b):
                pool.wait_ge(s_cThi, b + 1)
                pool.tensor_tensor(cT_lo[:], cT[:, b % 2], f32(cT_hi[:]), ALU.subtract).then_inc(s_cTlo, 1)

            def cw_store(b):
                pool.wait_ge(s_cwT, b + 1)
                pool.dma_start(cw_dram[:, b * L:(b + 1) * L], cwT[:]).then_inc(s_cwout[b], 16)

            rows_1 = (0, s_mv1, s_xn, s_ve1, s_rs1, s_sm1, s_sh1)
            rows_2 = (1, s_mv2, s_xn2, s_ve2, s_rs2, s_sm2, s_sh2)
            scale_shift(0, *rows_1)
            scale_shift(1, *rows_1)
            combine_k(0)
            ctx_lo(1)
            for b in range(B):
                if b + 2 < B:
                    scale_shift(b + 2, *rows_1)
                if b >= 2:
                    cw_store(b - 2)
                if b + 1 < B:
                    combine_k(b + 1)
                scale_shift(b, *rows_2)
                if b + 2 < B:
                    ctx_lo(b + 2)
            cw_store(B - 2)
            cw_store(B - 1)

            for n in range(4):
                pool.wait_ge(s_y, n + 1)
                rows = slice(n * HT // 2, (n + 1) * HT // 2)
                pool.dma_start(out[:, rows], x_sb[:, rows]).then_inc(s_store, 16)
            pool.wait_ge(s_store, 4 * 16)


def shape_constants(L, D):
    f = np.float32
    half = D // 2
    scale_vec = (np.arange(0, D, 2, dtype=f) + f(0.4 * D)) / f(1.4 * D)
    pos = np.arange(L, dtype=f)
    scale = scale_vec[None, :] ** (pos / f(SCALE_BASE))[:, None]
    freqs = f(1.0) / f(THETA) ** (np.arange(half, dtype=f) / f(half))
    angle = pos[:, None] * freqs[None, :]
    sin, cos = np.sin(angle), np.cos(angle)
    inverse = f(1.0) / scale
    rot_q = np.stack([(cos * scale).T, (sin * scale).T], axis=1)
    rot_k = np.stack([(cos * inverse).T, (sin * inverse).T], axis=1)
    diff = np.arange(L, dtype=f)[None, :] - np.arange(P, dtype=f)[:, None]
    decay = np.where(diff >= 0, f(GAMMA) ** np.maximum(diff, 0), f(0.0))
    return {"rot_q": rot_q.astype(f), "rot_k": rot_k.astype(f), "decay": decay.astype(f),
            "ident": np.eye(P, dtype=f)}


def laid_out(inputs):
    a = {k: np.asarray(v) for k, v in inputs.items()}
    x, ctx = a["x"], a["ctx_1024"]
    B, L, D = x.shape
    KT, LT = D // P, L // P
    E, _, H = a["L0_ffn_w1"].shape
    ES, _, HS = a["L0_ffn_sw1"].shape
    PAIR, CS = P // H, HS // P

    def rows_by_kt(w):
        return w.reshape(KT, P, w.shape[1]).transpose(1, 0, 2)

    def even_odd(w):
        return np.concatenate([w[:, 0::2], w[:, 1::2]], axis=1)

    wqkv = np.stack([rows_by_kt(even_odd(a["L0_xattn_Wq"])), rows_by_kt(even_odd(a["L0_xattn_Wk"])),
                     rows_by_kt(a["L0_xattn_Wv"])], axis=1)
    w1 = a["L0_ffn_w1"].reshape(E // PAIR, PAIR, KT, P, H).transpose(0, 3, 2, 1, 4).reshape(E // PAIR, P, KT * P)
    sw1 = a["L0_ffn_sw1"].reshape(ES, KT, P, CS, P).transpose(0, 3, 2, 1, 4).reshape(ES * CS, P, KT * P)
    w2 = a["L0_ffn_w2"].reshape(E // PAIR, P, D)
    sw2 = a["L0_ffn_sw2"].reshape(ES * CS, P, D)
    return {
        "x": x.reshape(B * LT, P, D).transpose(1, 0, 2),
        "ctxT": ctx.transpose(0, 2, 1).reshape(B, KT, P, L).transpose(0, 2, 1, 3),
        "wqkv": wqkv,
        "router_w": rows_by_kt(a["L0_ffn_router_w"]),
        "router_b": a["L0_ffn_router_b"],
        "w_ffn": np.concatenate([np.concatenate([w1, w2], axis=2), np.concatenate([sw1, sw2], axis=2)], axis=0),
        "b1T": np.concatenate([a["L0_ffn_b1"].reshape(-1, P), a["L0_ffn_sb1"].reshape(-1, P)], axis=0).T,
        "b2": a["L0_ffn_b2"],
        "sb2T": a["L0_ffn_sb2"].reshape(ES, KT, P).transpose(2, 0, 1),
    }


_NAMES = ["x", "ctxT", "wqkv", "router_w", "router_b", "w_ffn", "b1T", "b2", "sb2T",
          "ident", "rot_q", "rot_k", "decay"]


def kernel(**inputs):
    import concourse.bacc as bacc
    from concourse.bass_utils import run_bass_kernel_spmd

    B, L, D = inputs["x"].shape
    laid = laid_out(inputs)
    laid.update(shape_constants(L, D))
    nc = bacc.Bacc("TRN2", target_bir_lowering=False, num_devices=1)
    arrays, args = {}, []
    for name in _NAMES:
        a = np.ascontiguousarray(laid[name])
        arrays[f"in_{name}"] = a
        args.append(nc.dram_tensor(f"in_{name}", a.shape, mybir.dt.from_np(a.dtype), kind="ExternalInput").ap())
    out = nc.dram_tensor("out_rows", (P, B * L // P, D), F32, kind="ExternalOutput").ap()
    build(nc, *args, out)
    got = run_bass_kernel_spmd(nc, [arrays], core_ids=[0]).results[0]["out_rows"]
    return got.transpose(1, 0, 2).reshape(B, L, D)
```

```python
from contextlib import ExitStack

import numpy as np

import concourse.bass as bass
from concourse import mybir

F32 = mybir.dt.float32
F32R = mybir.dt.float32r
ALU = mybir.AluOpType
ACT = mybir.ActivationFunctionType
AX_X = mybir.AxisListType.X

P = 128
GAMMA, THETA, SCALE_BASE, EPS = 0.96875, 10000.0, 512.0, 1e-5
TOP = 8
WARM_UP = 10


def build(nc, x, ctxT, wqkv, router_w, router_b, w_ffn, b1T, b2, sb2T, ident, table_q, table_k, decay, out):
    _, BT, D = x.shape
    B, _, KT, L = ctxT.shape
    E = router_w.shape[2]
    CHUNKS = w_ffn.shape[0]
    TURNS = CHUNKS // 2
    ROUTED = E // 2
    H = P // 2
    LT = L // P
    T = B * L
    HALF = T // 2
    BLK = 512
    NBLK = HALF // BLK
    TILES = BLK // D
    BANKS = LT // TILES
    HT = HALF // P
    assert 2 * E == P and D == 256 and KT == 2 and L == BLK and NBLK == 2 and B == 2 * NBLK and BT == B * LT

    cw_dram = nc.dram_tensor("cw_by_expert", [E, T], F32, kind="Internal").ap()

    with ExitStack() as st:
        def sb(name, shape, dt=F32):
            return st.enter_context(nc.sbuf_tensor(name, shape, dt))

        def sem(name):
            return st.enter_context(nc.semaphore(name))

        ps = [st.enter_context(nc.psum_tensor(f"ps{i}", [P, 2, BLK], F32)) for i in range(4)]

        x_sb = sb("x_sb", [P, BT, D])
        xn_hi = sb("xn_hi", [P, KT, T], F32R)
        xn_lo = sb("xn_lo", [P, KT, T], F32R)
        id_sb = sb("id_sb", [P, P])
        cT = sb("cT", [P, 2, KT, L])
        tabq_sb = sb("tabq_sb", [P, 2, L])
        tabk_sb = sb("tabk_sb", [P, 2, L])
        decay_sb = sb("decay_sb", [P, L])
        w_raw = sb("w_raw", [P, 3, KT, D])
        w_hi = sb("w_hi", [P, 3, KT, D], F32R)
        w_lo = sb("w_lo", [P, 3, KT, D], F32R)
        rw_raw = sb("rw_raw", [P, KT, E])
        rw = sb("rw", [P, KT, 2, E], F32R)
        rb_sb = sb("rb_sb", [P, E])
        xn = sb("xn", [P, LT, D])
        xn2 = sb("xn2", [P, LT, D])
        xT_hi = sb("xT_hi", [P, KT, L], F32R)
        xT_lo = sb("xT_lo", [P, KT, L], F32R)
        cT_hi = sb("cT_hi", [P, KT, L], F32R)
        cT_lo = sb("cT_lo", [P, KT, L], F32R)
        outT = sb("outT", [P, KT, HALF])
        cwb = sb("cwb", [P, 2, HALF])
        rot_q = [outT[:, i, :].rearrange("p (s l) -> p s l", l=L) for i in range(2)]
        rot_k = [cwb[:, i, :].rearrange("p (s l) -> p s l", l=L) for i in range(2)]
        v = sb("v", [P, LT, D])
        SOFF = [sum(L - P * j for j in range(m)) for m in range(LT + 1)]
        sc = sb("sc", [P, SOFF[LT]])
        stats = sb("stats", [P, 2, LT, 6])
        mv = sb("mv", [P, 2, LT, 2])
        veps = sb("veps", [P, 2, LT])
        zeros = sc[:, 0:D]
        neg_mean = sb("neg_mean", [P, 2, LT])
        minus_half = sb("minus_half", [P, LT])
        rstd = sb("rstd", [P, 2, LT])
        shift = sb("shift", [P, 2, LT])
        lg = sb("lg", [P, 2, LT, E])
        lmax = sb("lmax", [P, LT])
        lsh = sb("lsh", [P, 2, LT, E])
        ex = sb("ex", [P, 2, LT, E])
        top = sb("top", [P, LT, TOP])
        rest = sb("rest", [P, LT, E])
        sel = sb("sel", [P, LT, E])
        tsum = sb("tsum", [P, LT])
        rsum = sb("rsum", [P, LT])
        cw = sb("cw", [P, 2, LT, 2 * E])
        cwT = sb("cwT", [E, 2, L])
        cw_hi = sb("cw_hi", [P, T], F32R)
        cw_lo = sb("cw_lo", [E, T], F32R)
        h_hi = sb("h_hi", [P, 2, NBLK, BLK], F32R)
        h_lo = sb("h_lo", [P, 2, NBLK, BLK], F32R)
        h = sb("h", [P, 2, NBLK, BLK])
        q, k_ = h[:, 0], h[:, 1]
        w1_raw = sb("w1_raw", [P, 2, KT, P])
        w2_raw = sb("w2_raw", [P, 2, D])
        w1_hi = sb("w1_hi", [P, 2, KT, P], F32R)
        w1_lo = sb("w1_lo", [P, 2, KT, P], F32R)
        w2_hi = sb("w2_hi", [P, 2, D], F32R)
        w2_lo = sb("w2_lo", [P, 2, D], F32R)
        b1_sb = sb("b1_sb", [P, NBLK, CHUNKS])
        sb2_sb = sb("sb2_sb", [P, 2, KT])
        sb2s = sb("sb2s", [P, KT])
        b2_raw = sb("b2_raw", [P, D])
        b2_hi = sb("b2_hi", [P, D], F32R)
        b2_hilo = sb("b2_hilo", [P, D], F32R)

        s_ident, s_tabq, s_tabk, s_decay = sem("s_ident"), sem("s_tabq"), sem("s_tabk"), sem("s_decay")
        s_w = [sem(f"s_win{i}") for i in range(3)]
        s_rw, s_rb, s_small = sem("s_rw"), sem("s_rb"), sem("s_small")
        s_x0 = [sem(f"s_x0in{i}") for i in range(2)]
        s_x = {b: sem(f"s_xin{b}") for b in range(1, B)}
        s_ctx = [sem(f"s_ctxin{b}") for b in range(B)]
        s_whi, s_wlo, s_wvlo, s_rwhi, s_rwlo = sem("s_whi"), sem("s_wlo"), sem("s_wvlo"), sem("s_rwhi"), sem("s_rwlo")
        s_mh, s_sb2s, s_zeros = sem("s_mh"), sem("s_sb2s"), sem("s_zeros")
        s_b2hi, s_b2hilo = sem("s_b2hi"), sem("s_b2hilo")
        s_st1, s_mv1, s_ve1, s_rs1, s_sh1, s_xn = (
            sem("s_st1"), sem("s_mv1"), sem("s_ve1"), sem("s_rs1"), sem("s_sh1"), sem("s_xn"))
        s_pxT, s_xThi, s_xTlo = sem("s_pxT"), sem("s_xThi"), sem("s_xTlo")
        s_cThi, s_cTlo = sem("s_cThi"), sem("s_cTlo")
        s_cThi0, s_cTlo0 = sem("s_cThi0"), sem("s_cTlo0")
        s_pq, s_pk, s_pv = sem("s_pq"), sem("s_pk"), sem("s_pv")
        s_rotq, s_rotk, s_k, s_v = sem("s_rotq"), sem("s_rotk"), sem("s_k"), sem("s_v")
        s_q0, s_q = sem("s_q0"), sem("s_q")
        s_ps, s_sc = sem("s_ps"), sem("s_sc")
        s_po, s_x2 = sem("s_po"), sem("s_x2")
        s_st2, s_mv2, s_ve2, s_rs2, s_sh2, s_xn2 = (
            sem("s_st2"), sem("s_mv2"), sem("s_ve2"), sem("s_rs2"), sem("s_sh2"), sem("s_xn2"))
        s_xn2_last = sem("s_xn2_last")
        s_px2T, s_x2Thi, s_x2Tlo = sem("s_px2T"), sem("s_x2Thi"), sem("s_x2Tlo")
        s_lgp = sem("s_lgp")
        s_plg, s_lg, s_lmax, s_lsh, s_ex = sem("s_plg"), sem("s_lg"), sem("s_lmax"), sem("s_lsh"), sem("s_ex")
        s_top, s_rest, s_sel, s_tsum, s_rsum, s_cw = (
            sem("s_top"), sem("s_rest"), sem("s_sel"), sem("s_tsum"), sem("s_rsum"), sem("s_cw"))
        s_pcw, s_cwT, s_cwhi, s_cwlo = sem("s_pcw"), sem("s_cwT"), sem("s_cwhi"), sem("s_cwlo")
        s_cwout = [sem(f"s_cwout{b}") for b in range(B)]
        s_w1in = [sem(f"s_w1in{i}") for i in range(2)]
        s_w2in = [sem(f"s_w2in{i}") for i in range(2)]
        s_cwb = [sem(f"s_cwbin{i}") for i in range(2)]
        s_w1hi, s_w1lo, s_w2hi, s_w2lo = sem("s_w1hi"), sem("s_w1lo"), sem("s_w2hi"), sem("s_w2lo")
        s_up, s_silu, s_hcw, s_hhi, s_hlo, s_down = (
            sem("s_up"), sem("s_silu"), sem("s_hcw"), sem("s_hhi"), sem("s_hlo"), sem("s_down"))
        s_sums, s_pout, s_y = sem("s_sums"), sem("s_pout"), sem("s_y")
        s_store = [sem(f"s_store{half}") for half in range(2)]
        s_outT = [sem(f"s_outT{k}") for k in range(KT)]

        def f32(ap):
            return ap.bitcast(F32)

        def three(pe, dst, l_hi, l_lo, r_hi, r_lo, first, last):
            pe.matmul(dst, l_hi, r_lo, start=first, stop=False)
            pe.matmul(dst, l_lo, r_hi, start=False, stop=False)
            return pe.matmul(dst, l_hi, r_hi, start=False, stop=last)

        def score_ps(m):
            n = L - m * P
            return ps[0][:, m, 0:n] if m < 2 else ps[1][:, 0, (m - 2) * 2 * P:(m - 2) * 2 * P + n]

        def over_chunks(eng, half, step):
            step(half, 0, True, False)
            with eng.Fori(1, ROUTED // 2) as i:
                step(half, i, False, False)
            step(half, ROUTED // 2, False, True)
            with eng.Fori(ROUTED // 2 + 1, TURNS - 1) as i:
                step(half, i, False, True)
            step(half, TURNS - 1, False, True)

        block = st.enter_context(nc.Block())

        @block.sync
        def _(sp):
            def load_x(b):
                sp.dma_start(x_sb[:, b * LT:(b + 1) * LT, :], x[:, b * LT:(b + 1) * LT, :]).then_inc(s_x[b], 16)

            def load_w(i):
                sp.dma_start(w_raw[:, i], wqkv[:, i]).then_inc(s_w[i], 16)

            for i in range(2):
                rows = slice(i * LT // 2, (i + 1) * LT // 2)
                sp.dma_start(x_sb[:, rows, :], x[:, rows, :]).then_inc(s_x0[i], 16)
            load_w(1)
            load_w(0)
            sp.dma_start(cT[:, 0], ctxT[0]).then_inc(s_ctx[0], 16)
            sp.dma_start(id_sb[:], ident).then_inc(s_ident, 16)
            load_x(1)
            load_w(2)
            sp.dma_start(tabk_sb[:], table_k).then_inc(s_tabk, 16)
            sp.dma_start(tabq_sb[:], table_q).then_inc(s_tabq, 16)
            sp.dma_start(cT[:, 1], ctxT[1]).then_inc(s_ctx[1], 16)
            sp.dma_start(decay_sb[:], decay).then_inc(s_decay, 16)
            sp.dma_start(rw_raw[:], router_w).then_inc(s_rw, 16)
            sp.dma_start(rb_sb[:], router_b.partition_broadcast(P)).then_inc(s_rb, 16)
            for i in range(NBLK):
                sp.dma_start(b1_sb[:, i], b1T).then_inc(s_small, 16)
            sp.dma_start(sb2_sb[:], sb2T).then_inc(s_small, 16)
            for i in range(2):
                sp.dma_start(b2_raw[i * E:(i + 1) * E, :], b2).then_inc(s_small, 16)
            for b in range(2, B):
                load_x(b)
                if b == 2:
                    sp.wait_ge(s_cTlo0, 1)
                else:
                    sp.wait_ge(s_cTlo, b - 2)
                sp.dma_start(cT[:, b % 2], ctxT[b]).then_inc(s_ctx[b], 16)

            def load_w1(c, slot):
                sp.dma_start(w1_raw[:, slot], w_ffn[bass.ds(c, 1), :, 0:KT * P]
                             .rearrange("o p (k h) -> p (o k) h", k=KT)).then_inc(s_w1in[slot], 16)

            def step(half, i, first, shared):
                for slot in range(2):
                    c = i * 2 + slot
                    g = c + half * CHUNKS
                    ahead = (c + 1) % CHUNKS if isinstance(c, int) else c + 1
                    if not (half and isinstance(c, int) and c == CHUNKS - 1):
                        if not (half == 0 and first and slot == 0):
                            sp.wait_ge(s_w1lo, g)
                        load_w1(ahead, 1 - slot)
                    if not (first and half == 0):
                        sp.wait_ge(s_w2lo, g - 1)
                    sp.dma_start(w2_raw[:, slot], w_ffn[bass.ds(c, 1), :, KT * P:]
                                 .rearrange("o p n -> p (o n)")).then_inc(s_w2in[slot], 16)
                    if shared:
                        continue
                    if first and slot == 0:
                        for b in range(half * NBLK, (half + 1) * NBLK):
                            sp.wait_ge(s_cwout[b], 16)
                        if half == 0:
                            sp.wait_ge(s_k, B)
                    if not (first and half == 0):
                        sp.wait_ge(s_hcw, NBLK * (c + half * ROUTED - 1))
                    for e in range(2):
                        sp.dma_start(cwb[e * H:(e + 1) * H, slot, :],
                                     cw_dram[bass.ds(c * 2 + e, 1), half * HALF:(half + 1) * HALF]
                                     .broadcast_to([H, HALF])).then_inc(s_cwb[slot], 16)
            load_w1(0, 0)
            for half in range(2):
                over_chunks(sp, half, step)
            for i in range(NBLK * BANKS, 2 * NBLK * BANKS):
                sp.wait_ge(s_y, i + 1)
                rows = slice(i * TILES, (i + 1) * TILES)
                sp.dma_start(out[:, rows], x_sb[:, rows]).then_inc(s_store[1], 16)
            sp.wait_ge(s_store[1], 16 * NBLK * BANKS)

        @block.tensor
        def _(pe):
            def transpose_x(b, dst):
                for t in range(LT):
                    pe.wait_ge(s_xn, LT * b + t + 1)
                    for k in range(KT):
                        last = pe.transpose(dst[:, k, t * P:(t + 1) * P], xn[:, t, k * P:(k + 1) * P], id_sb[:])
                last.then_inc(s_pxT, 1)

            def project(which, dst, src_hi, src_lo, done):
                for par in range(2):
                    for k in range(KT):
                        cols = slice(par * P, (par + 1) * P)
                        last = three(pe, dst[:, par, :], w_hi[:, which, k, cols], w_lo[:, which, k, cols],
                                     src_hi[:, k, :], src_lo[:, k, :], k == 0, k == KT - 1)
                last.then_inc(done, 1)

            def project_q(b):
                pe.wait_ge(s_xTlo, b + 1)
                if b >= 1:
                    pe.wait_ge(s_sc, 2 * b - 1)
                project(0, ps[0], xT_hi, xT_lo, s_pq)

            def project_k(b):
                if b == 0:
                    pe.wait_ge(s_cTlo0, 1)
                else:
                    pe.wait_ge(s_cTlo, b)
                if b >= 1:
                    pe.wait_ge(s_sc, 2 * b)
                project(1, ps[1], cT_hi, cT_lo, s_pk)

            def project_v(b):
                if b >= 1:
                    pe.wait_ge(s_x2, b)
                for t in range(LT):
                    for k in range(KT):
                        rows = slice(t * P, (t + 1) * P)
                        last = three(pe, ps[3][:, t // 2, (t % 2) * D:(t % 2 + 1) * D], cT_hi[:, k, rows],
                                     cT_lo[:, k, rows], w_hi[:, 2, k, :], w_lo[:, 2, k, :], k == 0, k == KT - 1)
                last.then_inc(s_pv, 1)

            def scores(b, pair):
                for m in (2 * pair, 2 * pair + 1):
                    for par in range(2):
                        last = pe.matmul(score_ps(m), k_[:, par, m * P:(m + 1) * P], q[:, par, m * P:L],
                                         start=par == 0, stop=par == 1)
                last.then_inc(s_ps, 1)

            def attend(b):
                pe.wait_ge(s_sc, 2 * b + 2)
                pe.wait_ge(s_v, b + 1)
                for t in range(LT):
                    for m in range(t + 1):
                        at = SOFF[m] + (t - m) * P
                        last = pe.matmul(ps[3][:, t // 2, (t % 2) * D:(t % 2 + 1) * D], sc[:, at:at + P],
                                         v[:, m, :], start=m == 0, stop=m == t)
                last.then_inc(s_po, 1)

            def transpose_x2(b):
                if b >= 1:
                    pe.wait_ge(s_lg, b)
                if b == 2:
                    pe.wait_ge(s_cwlo, b - 1)
                for t in range(LT):
                    if b < B - 1:
                        pe.wait_ge(s_xn2, LT * b + t + 1)
                    else:
                        pe.wait_ge(s_xn2_last, t + 1)
                    for k in range(KT):
                        last = pe.transpose(ps[2][:, k, t * P:(t + 1) * P], xn2[:, t, k * P:(k + 1) * P], id_sb[:])
                last.then_inc(s_px2T, 1)

            def logits(b):
                pe.wait_ge(s_x2Tlo, b + 1)
                if b == 0:
                    pe.wait_ge(s_rwlo, 1)
                for t in range(LT):
                    rows = slice(b * L + t * P, b * L + (t + 1) * P)
                    dst = ps[2][:, 0, t * 2 * E:(t + 1) * 2 * E]
                    for k in range(KT):
                        pe.matmul(dst, xn_hi[:, k, rows], rw[:, k].rearrange("p h e -> p (h e)"),
                                  start=k == 0, stop=False)
                        last = pe.matmul(dst[:, 0:E], xn_lo[:, k, rows], rw[:, k, 0, :],
                                         start=False, stop=k == KT - 1)
                last.then_inc(s_plg, 1)

            def transpose_cw(b, dst):
                pe.wait_ge(s_cw, b + 1)
                for t in range(LT):
                    last = pe.transpose(dst[:, t * P:(t + 1) * P], cw[:, b % 2, t], id_sb[:])
                last.then_inc(s_pcw, 1)

            pe.wait_ge(s_zeros, 1)
            for _ in range(WARM_UP):
                pe.matmul(ps[3][:, 0, 0:D], zeros[:, 0:P], zeros[:], start=True, stop=True)
            pe.wait_ge(s_ident, 16)
            transpose_x(0, ps[2])
            pe.wait_ge(s_wlo, 1)
            project_k(0)
            pe.wait_ge(s_wlo, 2)
            project_q(0)
            pe.wait_ge(s_wvlo, 1)
            project_v(0)
            pe.wait_ge(s_rotk, 1)
            transpose_x(1, ps[1])
            for b in range(B):
                if b == 0:
                    pe.wait_ge(s_q0, 1)
                else:
                    pe.wait_ge(s_q, b)
                pe.wait_ge(s_k, b + 1)
                scores(b, 0)
                pe.wait_ge(s_xTlo, min(b + 2, B))
                scores(b, 1)
                if b + 1 < B:
                    project_q(b + 1)
                else:
                    transpose_cw(b - 2, ps[1][:, 1, :])
                if b >= 1:
                    transpose_x2(b - 1)
                if b + 1 < B:
                    project_k(b + 1)
                attend(b)
                if 2 <= b < B - 1:
                    pe.wait_ge(s_x2Tlo, b)
                    transpose_cw(b - 2, ps[2][:, 1, :])
                if b >= 1:
                    logits(b - 1)
                if b + 2 < B:
                    pe.wait_ge(s_rotk, b + 2)
                    transpose_x(b + 2, ps[1])
                if b + 1 < B:
                    project_v(b + 1)

            def up(half, slot, n):
                cols = slice(half * HALF + n * BLK, half * HALF + (n + 1) * BLK)
                for k in range(KT):
                    last = three(pe, ps[slot][:, n, :], w1_hi[:, slot, k, :], w1_lo[:, slot, k, :],
                                 xn_hi[:, k, cols], xn_lo[:, k, cols], k == 0, k == KT - 1)
                last.then_inc(s_up, 1)

            def down_part(slot, g, k, n, end):
                cols = slice(k * P, (k + 1) * P)
                return three(pe, ps[2 + k][:, n, :], w2_hi[:, slot, cols], w2_lo[:, slot, cols],
                             h_hi[:, slot, n, :], h_lo[:, slot, n, :], False, end)

            def down(slot, g, end):
                pe.wait_ge(s_w2lo, g + 1)
                for n in range(NBLK):
                    pe.wait_ge(s_hlo, NBLK * g + n + 1)
                    for k in range(KT):
                        last = down_part(slot, g, k, n, end)
                    if end and n == 0:
                        last.then_inc(s_sums, 1)
                last.then_inc(s_down, 1)

            def bias(half, k):
                for n in range(NBLK):
                    rows = slice(half * HALF + n * BLK, half * HALF + (n + 1) * BLK)
                    dst, cols = ps[2 + k][:, n, :], slice(k * P, (k + 1) * P)
                    pe.matmul(dst, b2_hilo[:, cols], cw_hi[:, rows], start=True, stop=False)
                    pe.matmul(dst, b2_hilo[0:E, cols], cw_lo[:, rows], start=False, stop=False)

            def output(half):
                pe.wait_ge(s_silu, NBLK * (half + 1) * CHUNKS)
                for n in range(NBLK):
                    for k in range(KT):
                        pe.wait_ge(s_outT[k], NBLK * half + n + 1)
                    for a in range(BANKS):
                        for t in range(TILES):
                            for k in range(KT):
                                at = n * BLK + (a * TILES + t) * P
                                last = pe.transpose(ps[1 + n][:, a, t * D + k * P:t * D + (k + 1) * P],
                                                    outT[:, k, at:at + P], id_sb[:])
                        last.then_inc(s_pout, 1)

            def first_down():
                pe.wait_ge(s_x2, B)
                pe.wait_ge(s_b2hilo, 2)
                bias(0, 1)
                pe.wait_ge(s_w2lo, 1)
                pe.wait_ge(s_hlo, 1)
                down_part(0, 0, 1, 0, False)
                logits(B - 1)
                pe.wait_ge(s_hlo, 2)
                down_part(0, 0, 1, 1, False)
                pe.wait_ge(s_lg, B)
                bias(0, 0)
                for n in range(NBLK):
                    last = down_part(0, 0, 0, n, False)
                last.then_inc(s_down, 1)

            def step(half, i, first, shared):
                for slot in range(2):
                    c = i * 2 + slot
                    g = c + half * CHUNKS
                    pe.wait_ge(s_w1lo, g + 1)
                    if not first:
                        pe.wait_ge(s_silu, NBLK * (g - 1))
                    elif half and slot == 0:
                        pe.wait_ge(s_cwhi, B)
                        pe.wait_ge(s_cwlo, B)
                    elif half:
                        pe.wait_ge(s_y, BANKS)
                    elif slot:
                        pe.wait_ge(s_cwlo, NBLK)
                    for n in range(NBLK):
                        if first and half == 0 and slot and n:
                            transpose_x2(B - 1)
                        up(half, slot, n)
                    if first and slot == 0:
                        if half:
                            output(0)
                            bias(half, 1)
                        continue
                    if first and half == 0:
                        first_down()
                        continue
                    if first:
                        pe.wait_ge(s_y, NBLK * BANKS)
                        bias(half, 0)
                    elif half == 0 and isinstance(c, int) and c == CHUNKS - 1:
                        pe.wait_ge(s_silu, NBLK * g)
                        for j in range(NBLK):
                            transpose_cw(NBLK + j, ps[0][:, j, :])
                    down(1 - slot, g - 1, False)

            for half in range(2):
                over_chunks(pe, half, step)
                down(1, (half + 1) * CHUNKS - 1, True)
            output(1)

        @block.scalar
        def _(act):
            def w_split(i):
                act.wait_ge(s_w[i], 16)
                act.copy(w_hi[:, i], w_raw[:, i]).then_inc(s_whi, 1)

            def ctx_hi(b):
                act.wait_ge(s_ctx[b], 16)
                act.wait_ge(s_pv, b)
                act.copy(cT_hi[:], cT[:, b % 2]).then_inc(s_cThi, 1)

            def x_hi(b, src):
                act.wait_ge(s_pxT, b + 1)
                if b >= 1:
                    act.wait_ge(s_pq, b)
                act.copy(xT_hi[:], src[:]).then_inc(s_xThi, 1)

            def normalise(b, which, dst, s_shift, s_used, s_done):
                act.wait_ge(s_shift, b + 1)
                if b >= 1:
                    act.wait_ge(s_used, b)
                for t in range(LT):
                    act.activation(dst[:, t, :], x_sb[:, b * LT + t, :], ACT.Identity,
                                   bias=shift[:, which, t:t + 1], scale=rstd[:, which, t:t + 1]).then_inc(s_done, 1)

            def v_copy(b):
                act.wait_ge(s_pv, b + 1)
                if b >= 1:
                    act.wait_ge(s_po, b)
                act.copy(v[:], ps[3][:].rearrange("p a (t d) -> p (a t) d", d=D)).then_inc(s_v, 1)

            def x2_hi(b):
                act.wait_ge(s_px2T, b + 1)
                act.copy(xn_hi[:, :, b * L:(b + 1) * L], ps[2][:]).then_inc(s_x2Thi, 1)

            def exps(b):
                act.wait_ge(s_lsh, b + 1)
                if b >= 2:
                    act.wait_ge(s_sel, b - 1)
                act.activation(ex[:, b % 2], lsh[:, b % 2], ACT.Exp).then_inc(s_ex, 1)

            def cw_copy(b, src):
                act.wait_ge(s_pcw, b + 1)
                if b >= 2:
                    act.wait_ge(s_cwout[b - 2], 16)
                act.copy(cwT[:, b % 2], src[0:E, :]).then_inc(s_cwT, 1)

            def cw_split(b, src):
                act.copy(cw_hi[:, b * L:(b + 1) * L], src).then_inc(s_cwhi, 1)

            def w1_split(slot, load):
                act.wait_ge(s_w1in[slot], load * 16)
                act.copy(w1_hi[:, slot], w1_raw[:, slot]).then_inc(s_w1hi, 1)

            def w2_split(slot, load):
                act.wait_ge(s_w2in[slot], load * 16)
                act.copy(w2_hi[:, slot], w2_raw[:, slot]).then_inc(s_w2hi, 1)

            w_split(1)
            w_split(0)
            normalise(0, 0, xn, s_sh1, s_pxT, s_xn)
            x_hi(0, ps[2])
            w_split(2)
            normalise(1, 0, xn, s_sh1, s_pxT, s_xn)
            v_copy(0)
            x_hi(1, ps[1])
            ctx_hi(1)
            act.wait_ge(s_rw, 16)
            act.copy(rw[:, :, 0, :], rw_raw[:]).then_inc(s_rwhi, 1)
            act.wait_ge(s_small, 80)
            act.copy(b2_hi[:], b2_raw[:]).then_inc(s_b2hi, 1)
            act.copy(b2_hilo[0:E], b2_raw[0:E]).then_inc(s_b2hilo, 1)
            for b in range(B):
                if b == B - 1:
                    cw_copy(b - 2, ps[1][:, 1, :])
                if b >= 1:
                    x2_hi(b - 1)
                if b + 2 < B:
                    normalise(b + 2, 0, xn, s_sh1, s_pxT, s_xn)
                if b == B - 1:
                    cw_split(b - 2, ps[1][:, 1, :])
                if b == 1:
                    w1_split(0, 1)
                    w1_split(1, 1)
                    w2_split(0, 1)
                if 2 <= b < B - 1:
                    cw_copy(b - 2, ps[2][:, 1, :])
                    cw_split(b - 2, ps[2][:, 1, :])
                if b + 2 < B:
                    x_hi(b + 2, ps[1])
                if 1 <= b < B - 1:
                    exps(b - 1)
                if b + 1 < B:
                    v_copy(b + 1)
                if b + 2 < B:
                    ctx_hi(b + 2)
                if b == B - 1:
                    act.preload_act_table(ACT.Silu)
                if b < B - 1:
                    normalise(b, 1, xn2, s_sh2, s_px2T, s_xn2)

            def step(half, i, first, shared):
                for slot in range(2):
                    c = i * 2 + slot
                    g = c + half * CHUNKS
                    turn = i + half * TURNS
                    end = half and isinstance(c, int) and i == TURNS - 1
                    for n in range(NBLK):
                        act.wait_ge(s_up, NBLK * g + n + 1)
                        if first and half == 0:
                            act.wait_ge(s_ps, 2 * B)
                        else:
                            act.wait_ge(s_hlo, NBLK * (g - 2) + n + 1)
                        act.activation(h[:, slot, n], ps[slot][:, n, :], ACT.Silu,
                                       bias=b1_sb[:, n, bass.ds(c, 1)]).then_inc(s_silu, 1)
                    if not end:
                        w1_split(slot, turn + 2)
                    if half == 0 and isinstance(c, int) and c == CHUNKS - 1:
                        for j in range(NBLK):
                            cw_copy(NBLK + j, ps[0][:, j, :])
                    for n in range(NBLK):
                        if shared:
                            act.wait_ge(s_silu, NBLK * g + n + 1)
                        else:
                            act.wait_ge(s_hcw, NBLK * (c + half * ROUTED) + n + 1)
                        if not (first and half == 0):
                            act.wait_ge(s_down, g - 1)
                        act.copy(h_hi[:, slot, n], h[:, slot, n]).then_inc(s_hhi, 1)
                        if first and half == 0 and slot == 0 and n == 0:
                            x2_hi(B - 1)
                    if not (end and slot):
                        if not (first and half == 0 and slot == 0):
                            act.wait_ge(s_down, g)
                        w2_split(1 - slot, turn + 1 + slot)
                    if half == 0 and isinstance(i, int) and i == ROUTED // 2 and slot == 0:
                        for b in range(NBLK, B):
                            exps(b)
                        act.preload_act_table(ACT.Silu)

            for half in range(2):
                over_chunks(act, half, step)
                if half == 0:
                    for j in range(NBLK):
                        cw_split(NBLK + j, ps[0][:, j, :])
                if half:
                    act.wait_ge(s_pout, NBLK * BANKS)
                act.wait_ge(s_sb2s, 1)
                for n in range(NBLK):
                    if n == 0:
                        act.wait_ge(s_sums, half + 1)
                    else:
                        act.wait_ge(s_down, (half + 1) * CHUNKS)
                    act.activation(outT[:, 0, n * BLK:(n + 1) * BLK], ps[2][:, n, :], ACT.Identity,
                                   bias=sb2s[:, 0:1]).then_inc(s_outT[0], 1)

        @block.vector
        def _(dve):
            def stats_of(b, which, s_st, s_mv, s_ve, s_shift):
                if b >= 1:
                    dve.wait_ge(s_shift, b)
                for t in range(LT):
                    if b == 0 and which == 0 and t % (LT // 2) == 0:
                        dve.wait_ge(s_x0[t // (LT // 2)], 16)
                    dve.bn_stats(stats[:, which, t, :], x_sb[:, b * LT + t, :]).then_inc(s_st, 1)
                dve.wait_ge(s_st, LT * (b + 1))
                for t in range(LT):
                    dve.bn_aggr(mv[:, which, t, :], stats[:, which, t, :]).then_inc(s_mv, 1)
                dve.wait_ge(s_mv, LT * (b + 1))
                dve.tensor_scalar(neg_mean[:, which, :], mv[:, which, :, 0], -1.0, None, ALU.mult)
                dve.tensor_scalar(veps[:, which, :], mv[:, which, :, 1], EPS, None, ALU.add).then_inc(s_ve, 1)

            rows_1 = (0, s_st1, s_mv1, s_ve1, s_sh1)
            rows_2 = (1, s_st2, s_mv2, s_ve2, s_sh2)

            def w_rest(i, count):
                dve.wait_ge(s_whi, count)
                dve.tensor_tensor(w_lo[:, i], w_raw[:, i], f32(w_hi[:, i]), ALU.subtract).then_inc(s_wlo, 1)

            def x_lo(b, src):
                dve.wait_ge(s_xThi, b + 1)
                dve.tensor_tensor(xT_lo[:], src[:], f32(xT_hi[:]), ALU.subtract).then_inc(s_xTlo, 1)

            def rotate(src, table, rot, s_done):
                for par in range(2):
                    last = dve.tensor_tensor(rot[par], src[:, par:par + 1, :].broadcast_to([P, 2, L]), table[:],
                                             ALU.mult)
                last.then_inc(s_done, 1)

            def rotate_q(b):
                dve.wait_ge(s_pq, b + 1)
                if b >= 2:
                    dve.wait_ge(s_q, b - 1)
                rotate(ps[0], tabq_sb, rot_q, s_rotq)

            def rotate_k(b):
                dve.wait_ge(s_pk, b + 1)
                if b >= 1:
                    dve.wait_ge(s_k, b)
                rotate(ps[1], tabk_sb, rot_k, s_rotk)

            def decayed(b, pair):
                dve.wait_ge(s_ps, 2 * b + pair + 1)
                if b >= 1:
                    dve.wait_ge(s_po, b)
                for m in (2 * pair, 2 * pair + 1):
                    last = dve.tensor_tensor(sc[:, SOFF[m]:SOFF[m + 1]], score_ps(m), decay_sb[:, 0:L - m * P], ALU.mult)
                last.then_inc(s_sc, 1)

            def x2_lo(b):
                dve.wait_ge(s_x2Thi, b + 1)
                cols = slice(b * L, (b + 1) * L)
                dve.tensor_tensor(xn_lo[:, :, cols], ps[2][:], f32(xn_hi[:, :, cols]), ALU.subtract).then_inc(s_x2Tlo, 1)

            def route_0(b):
                dve.wait_ge(s_plg, b + 1)
                parts = ps[2][:, 0, :].rearrange("p (t h e) -> p t h e", h=2, e=E)
                dve.tensor_tensor(lg[:, b % 2], parts[:, :, 0, :], rb_sb[:].unsqueeze(1).broadcast_to([P, LT, E]),
                                  ALU.add).then_inc(s_lgp, 1)
                dve.wait_ge(s_lgp, b + 1)
                dve.tensor_tensor(lg[:, b % 2], parts[:, :, 1, :], lg[:, b % 2], ALU.add).then_inc(s_lg, 1)

            def route_1(b):
                dve.wait_ge(s_lg, b + 1)
                if b >= 1:
                    dve.wait_ge(s_lsh, b)
                dve.tensor_reduce(lmax[:], lg[:, b % 2], AX_X, ALU.max).then_inc(s_lmax, 1)
                dve.wait_ge(s_lmax, b + 1)
                dve.tensor_tensor(lsh[:, b % 2], lg[:, b % 2], lmax[:].unsqueeze(2).broadcast_to([P, LT, E]),
                                  ALU.subtract).then_inc(s_lsh, 1)

            def route_2(b):
                dve.wait_ge(s_ex, b + 1)
                for t in range(LT):
                    dve.max(top[:, t, :], ex[:, b % 2, t, :]).then_inc(s_top, 1)
                dve.wait_ge(s_top, LT * (b + 1))
                for t in range(LT):
                    dve.match_replace(rest[:, t, :], top[:, t, :], ex[:, b % 2, t, :], 0.0).then_inc(s_rest, 1)
                dve.tensor_reduce(tsum[:], top[:], AX_X, ALU.add).then_inc(s_tsum, 1)
                dve.wait_ge(s_rest, LT * (b + 1))
                dve.tensor_tensor(sel[:], ex[:, b % 2], rest[:], ALU.subtract).then_inc(s_sel, 1)
                dve.wait_ge(s_tsum, b + 1)
                dve.reciprocal(rsum[:], tsum[:]).then_inc(s_rsum, 1)
                dve.wait_ge(s_sel, b + 1)
                dve.wait_ge(s_rsum, b + 1)
                if b >= 2:
                    dve.wait_ge(s_pcw, b - 1)
                for i in range(2):
                    last = dve.tensor_tensor(cw[:, b % 2, :, i * E:(i + 1) * E], sel[:],
                                             rsum[:].unsqueeze(2).broadcast_to([P, LT, E]), ALU.mult)
                last.then_inc(s_cw, 1)

            def cw_rest(b, src):
                dve.wait_ge(s_cwhi, b + 1)
                cols = slice(b * L, (b + 1) * L)
                dve.tensor_tensor(cw_lo[:, cols], src[0:E, :], f32(cw_hi[0:E, cols]), ALU.subtract).then_inc(s_cwlo, 1)

            def attended(b):
                dve.wait_ge(s_po, b + 1)
                rows = x_sb[:, b * LT:(b + 1) * LT, :]
                dve.tensor_tensor(rows, ps[3][:].rearrange("p a (t d) -> p (a t) d", d=D), rows, ALU.add).then_inc(s_x2, 1)

            def attended_stats(b):
                dve.wait_ge(s_x2, b + 1)
                stats_of(b, *rows_2)

            def combine_q0():
                dve.wait_ge(s_rotq, 1)
                dve.tensor_tensor(q[:, 0, :], rot_q[0][:, 0, :], rot_q[1][:, 1, :], ALU.subtract)
                dve.tensor_tensor(q[:, 1, :], rot_q[0][:, 1, :], rot_q[1][:, 0, :], ALU.add).then_inc(s_q0, 1)

            def normalise_last():
                dve.wait_ge(s_sh2, B)
                dve.wait_ge(s_px2T, B - 1)
                for t in range(LT):
                    dve.tensor_scalar(xn2[:, t, :], x_sb[:, (B - 1) * LT + t, :], rstd[:, 1, t:t + 1],
                                      shift[:, 1, t:t + 1], ALU.mult, ALU.add).then_inc(s_xn2_last, 1)

            def w1_rest(slot, count):
                dve.wait_ge(s_w1hi, count)
                dve.tensor_tensor(w1_lo[:, slot], w1_raw[:, slot], f32(w1_hi[:, slot]), ALU.subtract).then_inc(s_w1lo, 1)

            def w2_rest(slot, count):
                dve.wait_ge(s_w2hi, count)
                dve.tensor_tensor(w2_lo[:, slot], w2_raw[:, slot], f32(w2_hi[:, slot]), ALU.subtract).then_inc(s_w2lo, 1)

            stats_of(0, *rows_1)
            w_rest(1, 1)
            w_rest(0, 2)
            dve.wait_ge(s_ctx[0], 16)
            dve.tensor_copy(cT_hi[:], cT[:, 0]).then_inc(s_cThi0, 1)
            dve.wait_ge(s_cThi0, 1)
            dve.tensor_tensor(cT_lo[:], cT[:, 0], f32(cT_hi[:]), ALU.subtract).then_inc(s_cTlo0, 1)
            dve.wait_ge(s_x[1], 16)
            stats_of(1, *rows_1)
            x_lo(0, ps[2])
            dve.wait_ge(s_tabk, 16)
            rotate_k(0)
            dve.wait_ge(s_tabq, 16)
            rotate_q(0)
            combine_q0()
            x_lo(1, ps[1])
            dve.wait_ge(s_rwhi, 1)
            dve.tensor_tensor(rw[:, :, 1, :], rw_raw[:], f32(rw[:, :, 0, :]), ALU.subtract).then_inc(s_rwlo, 1)
            dve.wait_ge(s_small, 80)
            dve.tensor_tensor(sb2s[:], sb2_sb[:, 0, :], sb2_sb[:, 1, :], ALU.add).then_inc(s_sb2s, 1)
            dve.wait_ge(s_b2hi, 1)
            dve.tensor_tensor(b2_hilo[E:2 * E], b2_raw[E:2 * E], f32(b2_hi[E:2 * E]), ALU.subtract).then_inc(s_b2hilo, 1)
            dve.wait_ge(s_decay, 16)
            dve.wait_ge(s_rb, 16)
            for b in range(B):
                decayed(b, 0)
                decayed(b, 1)
                if b + 2 < B:
                    dve.wait_ge(s_x[b + 2], 16)
                    stats_of(b + 2, *rows_1)
                if 2 <= b < B - 1:
                    route_2(b - 2)
                if b + 1 < B:
                    rotate_q(b + 1)
                if b >= 1:
                    x2_lo(b - 1)
                if b == B - 1:
                    cw_rest(b - 2, ps[1][:, 1, :])
                if b + 1 < B:
                    rotate_k(b + 1)
                if b == 1:
                    w1_rest(0, 1)
                    w1_rest(1, 2)
                    w2_rest(0, 1)
                attended(b)
                if b == B - 1:
                    attended_stats(b)
                if 2 <= b < B - 1:
                    cw_rest(b - 2, ps[2][:, 1, :])
                if b >= 1:
                    route_0(b - 1)
                if b < B - 1:
                    if b >= 1:
                        route_1(b - 1)
                    if b + 2 < B:
                        x_lo(b + 2, ps[1])
                    attended_stats(b)
                if b == B - 2:
                    route_2(b - 1)

            def to_rows(half, n):
                for a in range(BANKS):
                    done = (NBLK * half + n) * BANKS + a
                    dve.wait_ge(s_pout, done + 1)
                    rows = x_sb[:, done * TILES:(done + 1) * TILES, :]
                    dve.tensor_tensor(rows, ps[1 + n][:, a, :].rearrange("p (t d) -> p t d", d=D), rows,
                                      ALU.add).then_inc(s_y, 1)

            def step(half, i, first, shared):
                for slot in range(2):
                    c = i * 2 + slot
                    g = c + half * CHUNKS
                    end = half and isinstance(c, int) and i == TURNS - 1
                    if first and half and slot == 0:
                        to_rows(0, 0)
                    if not shared:
                        turn = i + half * (ROUTED // 2)
                        dve.wait_ge(s_cwb[slot], turn * 32 + 32)
                        for n in range(NBLK):
                            dve.wait_ge(s_silu, NBLK * g + n + 1)
                            dve.tensor_tensor(h[:, slot, n], h[:, slot, n], cwb[:, slot, n * BLK:(n + 1) * BLK],
                                              ALU.mult).then_inc(s_hcw, 1)
                            if first and half and slot == 0 and n:
                                to_rows(0, 1)
                            if first and half == 0 and slot == 0 and n == 0:
                                normalise_last()
                    if first and half == 0 and slot:
                        route_0(B - 1)
                    if not end:
                        w1_rest(slot, g + 3)
                    for n in range(NBLK):
                        dve.wait_ge(s_hhi, NBLK * g + n + 1)
                        dve.tensor_tensor(h_lo[:, slot, n], h[:, slot, n], f32(h_hi[:, slot, n]),
                                          ALU.subtract).then_inc(s_hlo, 1)
                        if first and half == 0 and slot == 0 and n == 0:
                            x2_lo(B - 1)
                    if not (end and slot):
                        w2_rest(1 - slot, g + 2)
                    if first and half == 0 and slot:
                        route_1(B - 2)
                        route_1(B - 1)
                    if half == 0 and isinstance(i, int) and i == ROUTED // 2:
                        route_2(NBLK + slot)

            for half in range(2):
                over_chunks(dve, half, step)
                if half == 0:
                    for j in range(NBLK):
                        cw_rest(NBLK + j, ps[0][:, j, :])
                if half:
                    dve.wait_ge(s_pout, NBLK * BANKS)
                for n in range(NBLK):
                    if n == 0:
                        dve.wait_ge(s_sums, half + 1)
                    else:
                        dve.wait_ge(s_down, (half + 1) * CHUNKS)
                    dve.tensor_scalar(outT[:, 1, n * BLK:(n + 1) * BLK], ps[3][:, n, :], sb2s[:, 1:2], None,
                                      ALU.add).then_inc(s_outT[1], 1)
            for n in range(NBLK):
                to_rows(1, n)

        @block.gpsimd
        def _(pool):
            pool.memset(zeros[:], 0.0).then_inc(s_zeros, 1)
            pool.memset(minus_half[:], -0.5).then_inc(s_mh, 1)
            pool.wait_ge(s_mh, 1)

            def scale_shift(b, which, s_ve, s_used, s_rs, s_shift):
                pool.wait_ge(s_ve, b + 1)
                if b >= 1:
                    pool.wait_ge(s_used, LT * b)
                pool.tensor_tensor(rstd[:, which, :], veps[:, which, :], minus_half[:], ALU.pow).then_inc(s_rs, 1)
                pool.wait_ge(s_rs, b + 1)
                pool.tensor_tensor(shift[:, which, :], neg_mean[:, which, :], rstd[:, which, :],
                                   ALU.mult).then_inc(s_shift, 1)

            rows_1 = (0, s_ve1, s_xn, s_rs1, s_sh1)
            rows_2 = (1, s_ve2, s_xn2, s_rs2, s_sh2)

            def combine_q(b):
                pool.wait_ge(s_rotq, b + 1)
                pool.wait_ge(s_ps, 2 * b)
                pool.tensor_tensor(q[:, 0, :], rot_q[0][:, 0, :], rot_q[1][:, 1, :], ALU.subtract)
                pool.tensor_tensor(q[:, 1, :], rot_q[0][:, 1, :], rot_q[1][:, 0, :], ALU.add).then_inc(s_q, 1)

            def combine_k(b):
                pool.wait_ge(s_rotk, b + 1)
                if b >= 1:
                    pool.wait_ge(s_ps, 2 * b)
                pool.tensor_tensor(k_[:, 0, :], rot_k[0][:, 0, :], rot_k[1][:, 1, :], ALU.subtract)
                pool.tensor_tensor(k_[:, 1, :], rot_k[0][:, 1, :], rot_k[1][:, 0, :], ALU.add).then_inc(s_k, 1)

            def ctx_lo(b):
                pool.wait_ge(s_cThi, b)
                pool.tensor_tensor(cT_lo[:], cT[:, b % 2], f32(cT_hi[:]), ALU.subtract).then_inc(s_cTlo, 1)

            def cw_store(b):
                pool.wait_ge(s_cwT, b + 1)
                pool.dma_start(cw_dram[:, b * L:(b + 1) * L], cwT[:, b % 2]).then_inc(s_cwout[b], 16)

            scale_shift(0, *rows_1)
            pool.wait_ge(s_whi, 3)
            pool.tensor_tensor(w_lo[:, 2], w_raw[:, 2], f32(w_hi[:, 2]), ALU.subtract).then_inc(s_wvlo, 1)
            scale_shift(1, *rows_1)
            combine_k(0)
            ctx_lo(1)
            for b in range(B):
                if b + 2 < B:
                    scale_shift(b + 2, *rows_1)
                if b + 1 < B:
                    combine_q(b + 1)
                    combine_k(b + 1)
                if b >= 2:
                    cw_store(b - 2)
                scale_shift(b, *rows_2)
                if b + 2 < B:
                    ctx_lo(b + 2)
            cw_store(B - 2)
            cw_store(B - 1)

            for n in range(NBLK):
                pool.wait_ge(s_y, (n + 1) * BANKS)
                rows = slice(n * LT, (n + 1) * LT)
                pool.dma_start(out[:, rows], x_sb[:, rows]).then_inc(s_store[0], 16)
            pool.wait_ge(s_store[0], 16 * NBLK)


def shape_constants(L, D):
    f = np.float32
    half = D // 2
    scale_vec = (np.arange(0, D, 2, dtype=f) + f(0.4 * D)) / f(1.4 * D)
    pos = np.arange(L, dtype=f)
    scale = scale_vec[None, :] ** (pos / f(SCALE_BASE))[:, None]
    freqs = f(1.0) / f(THETA) ** (np.arange(half, dtype=f) / f(half))
    angle = pos[:, None] * freqs[None, :]
    sin, cos = np.sin(angle), np.cos(angle)
    inverse = f(1.0) / scale
    rot_q = np.stack([(cos * scale).T, (sin * scale).T], axis=1)
    rot_k = np.stack([(cos * inverse).T, (sin * inverse).T], axis=1)
    diff = np.arange(L, dtype=f)[None, :] - np.arange(P, dtype=f)[:, None]
    decay = np.where(diff >= 0, f(GAMMA) ** np.maximum(diff, 0), f(0.0))
    return {"rot_q": rot_q.astype(f), "rot_k": rot_k.astype(f), "decay": decay.astype(f),
            "ident": np.eye(P, dtype=f)}


def laid_out(inputs):
    a = {k: np.asarray(v) for k, v in inputs.items()}
    x, ctx = a["x"], a["ctx_1024"]
    B, L, D = x.shape
    KT, LT = D // P, L // P
    E, _, H = a["L0_ffn_w1"].shape
    ES, _, HS = a["L0_ffn_sw1"].shape
    PAIR, CS = P // H, HS // P

    def rows_by_kt(w):
        return w.reshape(KT, P, w.shape[1]).transpose(1, 0, 2)

    def even_odd(w):
        return np.concatenate([w[:, 0::2], w[:, 1::2]], axis=1)

    wqkv = np.stack([rows_by_kt(even_odd(a["L0_xattn_Wq"])), rows_by_kt(even_odd(a["L0_xattn_Wk"])),
                     rows_by_kt(a["L0_xattn_Wv"])], axis=1)
    w1 = a["L0_ffn_w1"].reshape(E // PAIR, PAIR, KT, P, H).transpose(0, 3, 2, 1, 4).reshape(E // PAIR, P, KT * P)
    sw1 = a["L0_ffn_sw1"].reshape(ES, KT, P, CS, P).transpose(0, 3, 2, 1, 4).reshape(ES * CS, P, KT * P)
    w2 = a["L0_ffn_w2"].reshape(E // PAIR, P, D)
    sw2 = a["L0_ffn_sw2"].reshape(ES * CS, P, D)
    return {
        "x": x.reshape(B * LT, P, D).transpose(1, 0, 2),
        "ctxT": ctx.transpose(0, 2, 1).reshape(B, KT, P, L).transpose(0, 2, 1, 3),
        "wqkv": wqkv,
        "router_w": rows_by_kt(a["L0_ffn_router_w"]),
        "router_b": a["L0_ffn_router_b"],
        "w_ffn": np.concatenate([np.concatenate([w1, w2], axis=2), np.concatenate([sw1, sw2], axis=2)], axis=0),
        "b1T": np.concatenate([a["L0_ffn_b1"].reshape(-1, P), a["L0_ffn_sb1"].reshape(-1, P)], axis=0).T,
        "b2": a["L0_ffn_b2"],
        "sb2T": a["L0_ffn_sb2"].reshape(ES, KT, P).transpose(2, 0, 1),
    }


_NAMES = ["x", "ctxT", "wqkv", "router_w", "router_b", "w_ffn", "b1T", "b2", "sb2T",
          "ident", "rot_q", "rot_k", "decay"]


def kernel(**inputs):
    import concourse.bacc as bacc
    from concourse.bass_utils import run_bass_kernel_spmd

    B, L, D = inputs["x"].shape
    laid = laid_out(inputs)
    laid.update(shape_constants(L, D))
    nc = bacc.Bacc("TRN2", target_bir_lowering=False, num_devices=1)
    arrays, args = {}, []
    for name in _NAMES:
        a = np.ascontiguousarray(laid[name])
        arrays[f"in_{name}"] = a
        args.append(nc.dram_tensor(f"in_{name}", a.shape, mybir.dt.from_np(a.dtype), kind="ExternalInput").ap())
    out = nc.dram_tensor("out_rows", (P, B * L // P, D), F32, kind="ExternalOutput").ap()
    build(nc, *args, out)
    got = run_bass_kernel_spmd(nc, [arrays], core_ids=[0]).results[0]["out_rows"]
    return got.transpose(1, 0, 2).reshape(B, L, D)
```
